# Optimizing a Trainium2 kernel written in Bass

```python
import numpy as np
import jax
import jax.numpy as jnp

def _softmax(x, axis=-1):
    return jax.nn.softmax(x, axis=axis)

def _gelu(x):
    return jax.nn.gelu(x, approximate=True)

def _silu(x):
    return jax.nn.silu(x)

def _sigmoid(x):
    return jax.nn.sigmoid(x)

def _layernorm(x, axis=-1, eps=1e-05):
    m = jnp.mean(x, axis=axis, keepdims=True)
    v = jnp.var(x, axis=axis, keepdims=True)
    return (x - m) / jnp.sqrt(v + eps)

def _scatter_add(tgt, idx, src, axis=0):
    return tgt.at[idx].add(src)

def _segment_sum(src, seg, n):
    return jax.ops.segment_sum(src, seg, n)
kernel_name = 'mk_gnn_resnorm_d1_gnn_r8_4009f9'

def setup_inputs(seed: int=0):
    np.random.seed(seed)
    _w = jnp.asarray

    def _rec_inputs():
        import jax
        import jax.numpy as jnp
        _gk = jax.random.key(seed)
        x = -0.0003713 + 1 * jax.random.normal(jax.random.fold_in(_gk, 1), (12500, 128), jnp.float32)
        src = jax.random.randint(jax.random.fold_in(_gk, 2), (200000,), 0, 12500, jnp.int32)
        dst = jax.random.randint(jax.random.fold_in(_gk, 3), (200000,), 0, 12500, jnp.int32)
        _o = jnp.argsort(dst, stable=True)
        src = src[_o]
        dst = dst[_o]
        return (x, src, dst)
    x, src, dst = _rec_inputs()

    def _L0_gnn_setup():
        import jax, jax.numpy as jnp
        import numpy as np
        N, D, H, C, F = (12500, 128, 4, 32, 512)
        E = 75000
        NEG_SLOPE = 0.2
        LN_EPS = 1e-05

        def gatv2(x, src, dst, wl, bl, wr, br, att, bias):
            xl = (x @ wl + bl).reshape(N, H, C)
            xr = (x @ wr + br).reshape(N, H, C)
            e = jax.nn.leaky_relu(xl[src] + xr[dst], NEG_SLOPE)
            alpha = jnp.einsum('ehc,hc->eh', e, att)
            amax = jax.ops.segment_max(alpha, dst, num_segments=N)
            ex = jnp.exp(alpha - amax[dst])
            denom = jax.ops.segment_sum(ex, dst, num_segments=N)
            a = ex / (denom[dst] + 1e-16)
            msg = xl[src] * a[:, :, None]
            out = jax.ops.segment_sum(msg, dst, num_segments=N)
            return out.reshape(N, H * C) + bias

        def layer_norm(x, g, b):
            mu = jnp.mean(x, axis=-1, keepdims=True)
            var = jnp.var(x, axis=-1, keepdims=True)
            return (x - mu) * jax.lax.rsqrt(var + LN_EPS) * g + b

        def ffn(x, w1, b1, w2, b2):
            return jax.nn.relu(x @ w1 + b1) @ w2 + b2
        key = jax.random.key(seed)
        ks = iter(jax.random.split(key, 32))
        nrm = lambda shape, s=0.05: jax.random.normal(next(ks), shape, dtype=jnp.float32) * s
        inp = {'x': jax.random.normal(next(ks), (N, D), dtype=jnp.float32), 'edge_index': jax.random.randint(next(ks), (2, E), 0, N, dtype=jnp.int64)}
        for p in ('c1', 'c2'):
            inp[p + '_wl'] = nrm((D, H * C))
            inp[p + '_bl'] = jnp.zeros((H * C,), jnp.float32)
            inp[p + '_wr'] = nrm((D, H * C))
            inp[p + '_br'] = jnp.zeros((H * C,), jnp.float32)
            inp[p + '_att'] = nrm((H, C))
            inp[p + '_bias'] = jnp.zeros((H * C,), jnp.float32)
        for p in ('f1', 'f2'):
            inp[p + '_w1'] = nrm((D, F))
            inp[p + '_b1'] = jnp.zeros((F,), jnp.float32)
            inp[p + '_w2'] = nrm((F, D))
            inp[p + '_b2'] = jnp.zeros((D,), jnp.float32)
        for p in ('ln1', 'ln2'):
            inp[p + '_g'] = jnp.ones((D,), jnp.float32)
            inp[p + '_b'] = jnp.zeros((D,), jnp.float32)
        return inp
    _L0_gnn_all = _L0_gnn_setup()
    _L0_gnn_in = {k: v for k, v in _L0_gnn_all.items() if k in ('c1_wl', 'c1_bl', 'c1_wr', 'c1_br', 'c1_att', 'c1_bias', 'c2_wl', 'c2_bl', 'c2_wr', 'c2_br', 'c2_att', 'c2_bias', 'f1_w1', 'f1_b1', 'f1_w2', 'f1_b2', 'f2_w1', 'f2_b1', 'f2_w2', 'f2_b2', 'ln1_g', 'ln1_b', 'ln2_g', 'ln2_b')}
    del _L0_gnn_all
    return {'x': x, 'src': src, 'dst': dst, 'L0_gnn_c1_wl': _L0_gnn_in['c1_wl'], 'L0_gnn_c1_bl': _L0_gnn_in['c1_bl'], 'L0_gnn_c1_wr': _L0_gnn_in['c1_wr'], 'L0_gnn_c1_br': _L0_gnn_in['c1_br'], 'L0_gnn_c1_att': _L0_gnn_in['c1_att'], 'L0_gnn_c1_bias': _L0_gnn_in['c1_bias'], 'L0_gnn_c2_wl': _L0_gnn_in['c2_wl'], 'L0_gnn_c2_bl': _L0_gnn_in['c2_bl'], 'L0_gnn_c2_wr': _L0_gnn_in['c2_wr'], 'L0_gnn_c2_br': _L0_gnn_in['c2_br'], 'L0_gnn_c2_att': _L0_gnn_in['c2_att'], 'L0_gnn_c2_bias': _L0_gnn_in['c2_bias'], 'L0_gnn_f1_w1': _L0_gnn_in['f1_w1'], 'L0_gnn_f1_b1': _L0_gnn_in['f1_b1'], 'L0_gnn_f1_w2': _L0_gnn_in['f1_w2'], 'L0_gnn_f1_b2': _L0_gnn_in['f1_b2'], 'L0_gnn_f2_w1': _L0_gnn_in['f2_w1'], 'L0_gnn_f2_b1': _L0_gnn_in['f2_b1'], 'L0_gnn_f2_w2': _L0_gnn_in['f2_w2'], 'L0_gnn_f2_b2': _L0_gnn_in['f2_b2'], 'L0_gnn_ln1_g': _L0_gnn_in['ln1_g'], 'L0_gnn_ln1_b': _L0_gnn_in['ln1_b'], 'L0_gnn_ln2_g': _L0_gnn_in['ln2_g'], 'L0_gnn_ln2_b': _L0_gnn_in['ln2_b']}

def reference(x, src, dst, L0_gnn_c1_wl, L0_gnn_c1_bl, L0_gnn_c1_wr, L0_gnn_c1_br, L0_gnn_c1_att, L0_gnn_c1_bias, L0_gnn_c2_wl, L0_gnn_c2_bl, L0_gnn_c2_wr, L0_gnn_c2_br, L0_gnn_c2_att, L0_gnn_c2_bias, L0_gnn_f1_w1, L0_gnn_f1_b1, L0_gnn_f1_w2, L0_gnn_f1_b2, L0_gnn_f2_w1, L0_gnn_f2_b1, L0_gnn_f2_w2, L0_gnn_f2_b2, L0_gnn_ln1_g, L0_gnn_ln1_b, L0_gnn_ln2_g, L0_gnn_ln2_b):
    import jax
    import jax.numpy as jnp

    def _L0_gnn_ref(x, edge_index, c1_wl, c1_bl, c1_wr, c1_br, c1_att, c1_bias, c2_wl, c2_bl, c2_wr, c2_br, c2_att, c2_bias, f1_w1, f1_b1, f1_w2, f1_b2, f2_w1, f2_b1, f2_w2, f2_b2, ln1_g, ln1_b, ln2_g, ln2_b):
        import jax, jax.numpy as jnp
        import numpy as np
        N, D, H, C, F = (12500, 128, 4, 32, 512)
        E = 75000
        NEG_SLOPE = 0.2
        LN_EPS = 1e-05

        def gatv2(x, src, dst, wl, bl, wr, br, att, bias):
            xl = (x @ wl + bl).reshape(N, H, C)
            xr = (x @ wr + br).reshape(N, H, C)
            e = jax.nn.leaky_relu(xl[src] + xr[dst], NEG_SLOPE)
            alpha = jnp.einsum('ehc,hc->eh', e, att)
            amax = jax.ops.segment_max(alpha, dst, num_segments=N)
            ex = jnp.exp(alpha - amax[dst])
            denom = jax.ops.segment_sum(ex, dst, num_segments=N)
            a = ex / (denom[dst] + 1e-16)
            msg = xl[src] * a[:, :, None]
            out = jax.ops.segment_sum(msg, dst, num_segments=N)
            return out.reshape(N, H * C) + bias

        def layer_norm(x, g, b):
            mu = jnp.mean(x, axis=-1, keepdims=True)
            var = jnp.var(x, axis=-1, keepdims=True)
            return (x - mu) * jax.lax.rsqrt(var + LN_EPS) * g + b

        def ffn(x, w1, b1, w2, b2):
            return jax.nn.relu(x @ w1 + b1) @ w2 + b2
        src, dst = (edge_index[0], edge_index[1])
        h = gatv2(x, src, dst, c1_wl, c1_bl, c1_wr, c1_br, c1_att, c1_bias)
        h = layer_norm(h + ffn(h, f1_w1, f1_b1, f1_w2, f1_b2), ln1_g, ln1_b)
        h = gatv2(h, src, dst, c2_wl, c2_bl, c2_wr, c2_br, c2_att, c2_bias)
        h = layer_norm(h + ffn(h, f2_w1, f2_b1, f2_w2, f2_b2), ln2_g, ln2_b)
        return h
    edge_index = jnp.stack([src, dst])
    x = _layernorm(x + _L0_gnn_ref(x, edge_index, L0_gnn_c1_wl, L0_gnn_c1_bl, L0_gnn_c1_wr, L0_gnn_c1_br, L0_gnn_c1_att, L0_gnn_c1_bias, L0_gnn_c2_wl, L0_gnn_c2_bl, L0_gnn_c2_wr, L0_gnn_c2_br, L0_gnn_c2_att, L0_gnn_c2_bias, L0_gnn_f1_w1, L0_gnn_f1_b1, L0_gnn_f1_w2, L0_gnn_f1_b2, L0_gnn_f2_w1, L0_gnn_f2_b1, L0_gnn_f2_w2, L0_gnn_f2_b2, L0_gnn_ln1_g, L0_gnn_ln1_b, L0_gnn_ln2_g, L0_gnn_ln2_b), axis=-1)
    return x

_drawn_inputs = setup_inputs


def setup_inputs(seed=0):
    import zlib

    import numpy as np

    out = dict(_drawn_inputs(seed))
    spreads = {'L0_gnn_c1_bl': (0.0, 0.1),
     'L0_gnn_c1_br': (0.0, 0.8),
     'L0_gnn_c1_bias': (0.0, 0.1),
     'L0_gnn_c2_bl': (0.0, 0.1),
     'L0_gnn_c2_br': (0.0, 0.8),
     'L0_gnn_c2_bias': (0.0, 0.1),
     'L0_gnn_f1_b1': (0.0, 0.1),
     'L0_gnn_f1_b2': (0.0, 0.1),
     'L0_gnn_f2_b1': (0.0, 0.1),
     'L0_gnn_f2_b2': (0.0, 0.1),
     'L0_gnn_ln1_g': (1.0, 0.2),
     'L0_gnn_ln1_b': (0.0, 0.1),
     'L0_gnn_ln2_g': (1.0, 0.2),
     'L0_gnn_ln2_b': (0.0, 0.1)}
    factors = {'L0_gnn_c1_wr': 8.0, 'L0_gnn_c2_wr': 8.0, 'L0_gnn_c2_att': 4.766}
    for name, (base, spread) in spreads.items():
        noise = np.random.default_rng([zlib.crc32(name.encode()), seed]).standard_normal(out[name].shape)
        drawn = base * np.exp(spread * noise) if base else spread * noise
        out[name] = jnp.asarray(drawn.astype(out[name].dtype))
    for name, factor in factors.items():
        out[name] = (out[name] * factor).astype(out[name].dtype)
    return out
```

```python
from contextlib import ExitStack

import concourse.bass as bass
from concourse import mybir

F32 = mybir.dt.float32
BF16 = mybir.dt.bfloat16
I32 = mybir.dt.int32
I16 = mybir.dt.int16
ALU = mybir.AluOpType
ACT = mybir.ActivationFunctionType
AX_X = mybir.AxisListType.X
DVE = mybir.EngineType.DVE
PE = mybir.EngineType.PE

P = 128
N = 12500
D = 128
H, C = 4, 32
F = 512
E = 200000
TILES = -(-N // P)
NP = TILES * P
CHUNKS = -(-E // P)
G = 16
SB = 13
STEPS = SB * P
GROUPS = STEPS // G
Q = 4
NQ = G // Q
W = D + H
RING = 3
BIG = 1.0e30
RESET = -1.0e38
EPS = 1e-5
SLOPE = 0.2
SLOT = G + 1
BT = 7
BATCHES = TILES // BT
FB = F // P
assert STEPS >= CHUNKS + TILES - 1 and GROUPS * G == STEPS and BATCHES * BT == TILES


def wait(eng, sem, value):
    if isinstance(value, int) and value <= 0:
        return
    eng.wait_ge(sem, value)


def hold(eng, sem, value, passed):
    wait(eng, sem, value)
    eng.sem_inc(passed, 1)


def build(nc, a, out):
    top = ExitStack()
    with top:
        def sb(name, shape, dt):
            return top.enter_context(nc.sbuf_tensor(name, shape, dt))

        def sem(name):
            return top.enter_context(nc.semaphore(name))

        xl_table = nc.dram_tensor("xl_table", [NP, D], F32).ap()
        flag_rows = nc.dram_tensor("flag_rows", [STEPS, 2 * P], BF16).ap()
        tile_of_step = nc.dram_tensor("tile_of_step", [SB, P], F32).ap()
        tile_offsets = nc.dram_tensor("tile_offsets", [2, STEPS + 1], I32).ap()

        m = {}
        m["xr3"] = sb("xr3", [P, TILES * 3 * D], BF16)
        m["sums"] = sb("sums", [P, TILES * W], F32)
        m["srcs"] = sb("srcs", [P, STEPS], I16)
        m["dloc"] = sb("dloc", [P, STEPS + G], BF16)
        m["resets"] = sb("resets", [P, STEPS], BF16)
        m["ident"] = sb("ident", [P, P], F32)
        m["iota_row"] = sb("iota_row", [P, P], F32)
        m["wproj"] = sb("wproj", [P, 2 * D], F32)
        m["bproj"] = sb("bproj", [P, 2 * D], F32)
        m["att"] = sb("att", [P, H], F32)
        WORK = 72704
        m["work"] = sb("work", [P, WORK // 4], F32)

        prepare(nc, a, m, flag_rows, tile_of_step, tile_offsets)
        project_input(nc, a, m, xl_table)
        edges(nc, a, m, 1, xl_table, flag_rows, tile_offsets)
        dense(nc, a, m, 1, xl_table, None)
        edges(nc, a, m, 2, xl_table, flag_rows, tile_offsets)
        dense(nc, a, m, 2, None, out)


class Area:

    def __init__(self, work):
        self.work, self.at = work, 0

    def take(self, columns, dt=F32):
        size = {F32: 4, I32: 4, BF16: 2, I16: 2}[dt]
        words = -(-columns * size // 4)
        v = self.work[:, self.at:self.at + words]
        self.at += words
        assert self.at <= self.work.shape[1], self.at
        return v if dt == F32 else v.bitcast(dt)[:, 0:columns]


def prepare(nc, a, m, flag_rows, tile_of_step, tile_offsets):
    ctx = ExitStack()
    with ctx:
        def sem(name):
            return ctx.enter_context(nc.semaphore("p_" + name))

        area = Area(m["work"])
        last_dst = area.take(CHUNKS, I32)
        end_tile = area.take(CHUNKS, I32)
        chunk_no = area.take(CHUNKS, I32)
        end_step = area.take(CHUNKS)
        chunk_f = area.take(CHUNKS)
        before = area.take(CHUNKS)
        step_i = area.take(SB, I32)
        step_no = area.take(SB)
        chunk_of = area.take(SB)
        tile_of = area.take(SB)
        tile_base = area.take(SB)
        chunk_idx = area.take(SB, I32)
        iota_i = area.take(P, I32)
        tcol = area.take(P)
        prep2 = area.at
        area2 = Area(m["work"])
        area2.at = prep2
        tiles_b = area.take(STEPS)
        trow = area.take(2 * (STEPS + 1), I32)
        src_i = m["sums"][:, 0:STEPS].bitcast(I32)
        dst_i = m["sums"][:, STEPS:2 * STEPS].bitcast(I32)
        src_f = m["sums"][:, 2 * STEPS:3 * STEPS]
        dst_f = m["sums"][:, 3 * STEPS:4 * STEPS]
        dloc_f = m["sums"][:, 4 * STEPS:5 * STEPS]
        flags = m["sums"][:, 5 * STEPS:6 * STEPS + STEPS].bitcast(BF16)[:, 0:2 * STEPS]
        ps = [ctx.enter_context(nc.psum_tensor(f"p_ps{i}", [P, 512], F32)) for i in range(2)]

        loaded, iotas, stair = sem("loaded"), sem("iotas"), sem("stair")
        ident0, gathered, tiles_out, tiles_in = sem("ident0"), sem("gathered"), sem("tiles_out"), sem("tiles_in")
        turned, moved, rows_out, flags_out, v = sem("turned"), sem("moved"), sem("rows_out"), sem("flags_out"), sem("v")
        tables, tT, tC = sem("tables"), sem("tT"), sem("tC")
        block = ctx.enter_context(nc.Block())

        @block.sync
        def _(sp):
            sp.dma_start(last_dst, a["last_dst"].partition_broadcast(P)).then_inc(loaded, 16)
            sp.wait_ge(tC, 1)
            sp.dma_start(tile_of_step, tcol[0:SB, :]).then_inc(tiles_out, 16)
            sp.wait_ge(tiles_out, 16)
            sp.dma_start(tiles_b, tile_of_step.rearrange("k p -> (k p)").partition_broadcast(P)).then_inc(tiles_in, 16)
            sp.wait_ge(rows_out, 1)
            sp.dma_start(tile_offsets.rearrange("a b -> (a b)").partition_broadcast(1), trow[0:1, :]).then_inc(flags_out, 16)
            sp.wait_ge(tables, 1)
            sp.dma_start(flag_rows.rearrange("(k p) f -> p k f", p=P),
                         flags.rearrange("p (k f) -> p k f", k=SB)).then_inc(flags_out, 16)
            sp.wait_ge(flags_out, 32)

        @block.gpsimd
        def _(pool):
            nc.gpsimd.iota(chunk_no, pattern=[[1, CHUNKS]], base=0, channel_multiplier=0).then_inc(iotas, 1)
            nc.gpsimd.iota(step_i, pattern=[[P, SB]], base=0, channel_multiplier=1).then_inc(iotas, 1)
            nc.gpsimd.iota(iota_i, pattern=[[1, P]], base=0, channel_multiplier=0).then_inc(iotas, 1)
            nc.gpsimd.memset(m["ident"][:, :], 0.0).then_inc(ident0, 1)
            pool.wait_ge(ident0, 1)
            nc.gpsimd.affine_select(out=m["ident"][:, :], in_=m["ident"][:, :], compare_op=ALU.not_equal,
                                    fill=1.0, base=0, pattern=[[-1, P]], channel_multiplier=1).then_inc(ident0, 1)
            pool.wait_ge(stair, 1)
            for k in range(SB):
                for rows, name in ((src_i, "src_chunks"), (dst_i, "dst_chunks")):
                    nc.gpsimd.indirect_dma_start(
                        out=rows[:, k * P:(k + 1) * P], out_offset=None, in_=a[name],
                        in_offset=bass.IndirectOffsetOnAxis(ap=chunk_idx[:, k:k + 1], axis=0)).then_inc(gathered, 16)
            pool.wait_ge(gathered, 32 * SB)

        @block.vector
        def _(dve):
            n = [0]

            def link(ins):
                n[0] += 1
                ins.then_inc(v, 1)
                dve.wait_ge(v, n[0])

            dve.wait_ge(iotas, 3)
            link(nc.vector.tensor_copy(m["iota_row"][:, :], iota_i))
            link(nc.vector.memset(m["dloc"][:, STEPS:], -1.0))
            link(nc.vector.tensor_copy(step_no, step_i))
            link(nc.vector.tensor_copy(chunk_f, chunk_no))
            dve.wait_ge(loaded, 16)
            link(nc.vector.tensor_scalar(end_tile, last_dst, 7, None, ALU.arith_shift_right))
            link(nc.vector.tensor_copy(end_step, end_tile))
            link(nc.vector.tensor_tensor(end_step, end_step, chunk_f, ALU.add))
            for k in range(SB):
                link(nc.vector.tensor_scalar(before, end_step, step_no[:, k:k + 1], None, ALU.is_lt))
                link(nc.vector.tensor_reduce(chunk_of[:, k:k + 1], before, axis=AX_X, op=ALU.add))
            link(nc.vector.tensor_tensor(tile_of, step_no, chunk_of, ALU.subtract))
            link(nc.vector.tensor_scalar(tile_of, tile_of, float(TILES - 1), None, ALU.min))
            link(nc.vector.tensor_scalar(tile_base, tile_of, float(P), None, ALU.mult))
            nc.vector.tensor_copy(chunk_idx, chunk_of).then_inc(stair, 1)
            dve.wait_ge(tT, 1)
            nc.vector.tensor_copy(tcol[0:SB, :], ps[0][0:SB, 0:P]).then_inc(tC, 1)
            dve.wait_ge(tiles_in, 16)
            link(nc.vector.memset(m["resets"][:, 0:1], 0.0))
            link(nc.vector.tensor_tensor(m["resets"][:, 1:STEPS], tiles_b[:, 1:STEPS], tiles_b[:, 0:STEPS - 1],
                                         ALU.not_equal))
            link(nc.vector.tensor_scalar(m["resets"][:, :], m["resets"][:, :], RESET, None, ALU.mult))
            link(nc.vector.memset(trow[0:1, :], 0))
            link(nc.vector.tensor_scalar(trow[0:1, 1:STEPS + 1], tiles_b[0:1, :], float(3 * D), None, ALU.mult))
            nc.vector.tensor_scalar(trow[0:1, STEPS + 2:2 * STEPS + 2], tiles_b[0:1, :], float(W), None,
                                    ALU.mult).then_inc(rows_out, 1)
            dve.wait_ge(gathered, 32 * SB)
            link(nc.vector.tensor_copy(src_f, src_i))
            link(nc.vector.tensor_copy(dst_f, dst_i))
            for k in range(SB):
                c = slice(k * P, (k + 1) * P)
                link(nc.vector.tensor_scalar(dloc_f[:, c], dst_f[:, c], tile_base[:, k:k + 1], None, ALU.subtract))
            d3 = dst_f.rearrange("p (k e) -> p k e", k=SB)
            f4 = flags.rearrange("p (k w e) -> p k w e", k=SB, w=2)
            link(nc.vector.tensor_tensor(f4[:, :, 0, 1:P], d3[:, :, 1:P], d3[:, :, 0:P - 1], ALU.not_equal))
            link(nc.vector.tensor_copy(f4[:, :, 1, 0:P - 1], f4[:, :, 0, 1:P]))
            link(nc.vector.memset(f4[:, :, 0, 0:1], 1.0))
            link(nc.vector.memset(f4[:, :, 1, P - 1:P], 1.0))
            nc.vector.tensor_scalar(f4[:, :, 0, :], f4[:, :, 0, :], RESET, None, ALU.mult).then_inc(tables, 1)
            nc.vector.tensor_copy(dloc_f[:, 0:1], dloc_f[:, 0:1]).then_inc(turned, 1)
            for k in range(SB):
                dve.wait_ge(moved, k + 1)
                c = slice(k * P, (k + 1) * P)
                link(nc.vector.tensor_copy(m["srcs"][:, c], ps[k % 2][:, 0:P]))
                nc.vector.tensor_copy(m["dloc"][:, c], ps[k % 2][:, P:2 * P]).then_inc(turned, 1)

        @block.tensor
        def _(pe):
            pe.wait_ge(ident0, 2)
            pe.wait_ge(stair, 1)
            nc.tensor.transpose(ps[0][0:SB, 0:P], tile_of, m["ident"][:, :]).then_inc(tT, 1)
            pe.wait_ge(tC, 1)
            for k in range(SB):
                pe.wait_ge(turned, max(1, k))
                c = slice(k * P, (k + 1) * P)
                nc.tensor.transpose(ps[k % 2][:, 0:P], src_f[:, c], m["ident"][:, :])
                nc.tensor.transpose(ps[k % 2][:, P:2 * P], dloc_f[:, c], m["ident"][:, :]).then_inc(moved, 1)


def load_projection(sp, a, m, layer, sem):
    c = f"c{layer}_"
    sp.dma_start(m["wproj"][:, 0:D], a[c + "wl"]).then_inc(sem, 16)
    sp.dma_start(m["wproj"][:, D:2 * D], a[c + "wr"]).then_inc(sem, 16)
    sp.dma_start(m["bproj"][:, 0:D], a[c + "bl"].partition_broadcast(P)).then_inc(sem, 16)
    sp.dma_start(m["bproj"][:, D:2 * D], a[c + "br"].partition_broadcast(P)).then_inc(sem, 16)
    for h in range(H):
        sp.dma_start(m["att"][h * C:(h + 1) * C, h:h + 1], a[c + "att"][h * C:(h + 1) * C, :]).then_inc(sem, 16)
    return 16 * (4 + H)


def parts_view(m):
    return m["xr3"][:, :].rearrange("p (t i d) -> p t i d", i=3, d=D)


def project_input(nc, a, m, xl_table):
    ctx = ExitStack()
    with ctx:
        def sem(name):
            return ctx.enter_context(nc.semaphore("i_" + name))

        area = Area(m["work"])
        xT = [area.take(BT * P) for _ in range(2)]
        both = [area.take(BT * 2 * D) for _ in range(2)]
        ps = [ctx.enter_context(nc.psum_tensor(f"i_ps{i}", [P, 512], F32)) for i in range(2)]
        w_in, x_in, att0 = sem("w_in"), [sem("x_in0"), sem("x_in1")], sem("att0")
        made, added, hi, mid, rest1, low, stored, both_free = (
            sem(s) for s in ("made", "added", "hi", "mid", "rest1", "low", "stored", "both_free"))
        block = ctx.enter_context(nc.Block())
        x3 = parts_view(m)

        @block.sync
        def _(sp):
            sp.wait_ge(att0, 1)
            load_projection(sp, a, m, 1, w_in)
            with sp.Fori(0, BATCHES // 2) as it:
                for b in range(2):
                    k = it * 2 + b
                    sp.wait_ge(made, k * BT + BT)
                    sp.dma_start(xT[b], a["xT"][:, bass.ds(k * (BT * P), BT * P)]).then_inc(x_in[b], 16)

        @block.gpsimd
        def _(pool):
            nc.gpsimd.memset(m["att"][:, :], 0.0).then_inc(att0, 1)
            with pool.Fori(0, BATCHES // 2) as it:
                for b in range(2):
                    k = it * 2 + b
                    pool.wait_ge(added, k * BT + (BT + 2))
                    pool.dma_start(xl_table[bass.ds(k * (BT * P), BT * P), :].rearrange("(t p) d -> p t d", p=P),
                                   both[b].rearrange("p (t d) -> p t d", t=BT)[:, :, 0:D]).then_inc(stored, 16)
                    pool.wait_ge(stored, k * 16 + 16)
                    pool.sem_inc(both_free, 1)

        @block.tensor
        def _(pe):
            pe.sem_inc(made, 2 * BT)
            pe.wait_ge(w_in, 16 * (4 + H))
            with pe.Fori(0, BATCHES // 2) as it:
                for b in range(2):
                    k = it * 2 + b
                    pe.wait_ge(x_in[b], it * 16 + 16)
                    for j in range(BT):
                        pe.wait_ge(added, k * BT + (j + 1))
                        nc.tensor.matmul(ps[(b * BT + j) % 2][:, 0:2 * D], xT[b][:, j * P:(j + 1) * P],
                                         m["wproj"][:, :], start=True, stop=True).then_inc(made, 1)

        @block.vector
        def _(dve):
            dve.sem_inc(added, 2)
            dve.sem_inc(both_free, 2)
            dve.sem_inc(low, 2)
            with dve.Fori(0, BATCHES // 2) as it:
                for b in range(2):
                    k = it * 2 + b
                    b3 = both[b].rearrange("p (t d) -> p t d", t=BT)
                    for j in range(BT):
                        dve.wait_ge(made, k * BT + (j + 1 + 2 * BT))
                        if j == 0:
                            dve.wait_ge(both_free, k + 1)
                            dve.wait_ge(low, k + 1)
                        nc.vector.tensor_tensor(b3[:, j, :], ps[(b * BT + j) % 2][:, 0:2 * D], m["bproj"][:, :],
                                                ALU.add).then_inc(added, 1)
                    rest = b3[:, :, D:2 * D]
                    tiles = bass.ds(k * BT, BT)
                    dve.wait_ge(hi, k + 1)
                    nc.vector.tensor_tensor(rest, rest, x3[:, tiles, 0, :], ALU.subtract).then_inc(rest1, 1)
                    dve.wait_ge(mid, k + 1)
                    nc.vector.tensor_tensor(x3[:, tiles, 2, :], rest, x3[:, tiles, 1, :], ALU.subtract).then_inc(low, 1)

        @block.scalar
        def _(act):
            with act.Fori(0, BATCHES // 2) as it:
                for b in range(2):
                    k = it * 2 + b
                    rest = both[b].rearrange("p (t d) -> p t d", t=BT)[:, :, D:2 * D]
                    tiles = bass.ds(k * BT, BT)
                    act.wait_ge(added, k * BT + (BT + 2))
                    nc.scalar.copy(x3[:, tiles, 0, :], rest).then_inc(hi, 1)
                    act.wait_ge(rest1, k + 1)
                    nc.scalar.copy(x3[:, tiles, 1, :], rest).then_inc(mid, 1)


def edges(nc, a, m, layer, xl_table, flag_rows, tile_offsets):
    ctx = ExitStack()
    with ctx:
        def sem(name):
            return ctx.enter_context(nc.semaphore(f"e{layer}_{name}"))

        def pb(name):
            return ctx.enter_context(nc.psum_tensor(f"e{layer}_{name}", [P, 512], F32))

        area = Area(m["work"])
        xg = [area.take(G * W).rearrange("p (s w) -> p s w", s=G) for _ in range(RING)]
        sel = [area.take(G * P).rearrange("p (s n) -> p s n", s=G) for _ in range(RING)]
        selT = [area.take(G * P, BF16).rearrange("p (s e) -> p s e", s=G) for _ in range(RING)]
        flags = [area.take(2 * P, BF16) for _ in range(RING)]
        idx = [area.take(G, I32) for _ in range(RING)]
        offs = [area.take(2 * SLOT, I32) for _ in range(RING)]
        z = [area.take(Q * P) for _ in range(2)]
        scores = area.take(G * H)
        running = area.take(P)
        last = area.take(P)
        lastT = area.take(G * (H + 1))
        absent = area.take(G)
        found = area.take(H * SLOT)
        upto = area.take(H * SLOT)
        upmax = area.take(H * SLOT)
        reset = area.take(H * SLOT + 1)
        rest = area.take(H * G)
        mx3 = area.take(G * 3 * H, BF16)
        mx = area.take(G * H)
        diff = area.take(G * H)
        grow = area.take(2 * H)
        z_ps = [pb("z0"), pb("z1")]
        t_ps = [pb("t0"), pb("t1")]
        score_ps, small_ps = pb("scores"), pb("small")
        o_ps = [pb("o0"), pb("o1")]
        turned_ps = small_ps[:, 0:P]
        lastT_ps = small_ps[:, P:P + G * (H + 1)]
        at = P + G * (H + 1)
        found_ps = small_ps[:, at:at + G * (H + 1)].rearrange("p (s k) -> p s k", k=H + 1)
        at += G * (H + 1)
        mx_ps = small_ps[:, at:at + G * 3 * H]

        gathered = [sem(f"gathered{b}") for b in range(RING)]
        control = [sem(f"control{b}") for b in range(RING)]
        idx_ready = sem("idx_ready")
        sel_built, selT_turned, selT_made = sem("sel_built"), sem("selT_turned"), sem("selT_made")
        z_summed, z_scaled, z_rect, z_scored = sem("z_summed"), sem("z_scaled"), sem("z_rect"), sem("z_scored")
        scores_kept, turned, last_made, last_turned, last_kept = (
            sem("scores_kept"), sem("turned"), sem("last_made"), sem("last_turned"), sem("last_kept"))
        found_made, mx_made, mx_picked, chain = sem("found_made"), sem("mx_made"), sem("mx_picked"), sem("chain")
        grow_in, grown, diff_made, weights = sem("grow_in"), sem("grown"), sem("diff_made"), sem("weights")
        messages, summed, folded, zeroed = sem("messages"), sem("summed"), sem("folded"), sem("zeroed")
        passed = sem("passed")
        CHAIN = 13
        FOLDS = G + 1
        block = ctx.enter_context(nc.Block())
        r0 = m["resets"]

        def over_groups(eng, body, head, tail):
            for g in range(head):
                body(g, g // RING, g % RING)
            loops = (tail - head) // RING
            with eng.Fori(0, loops) as it:
                for u in range(RING):
                    body(it * RING + (head + u), it + (head + u) // RING, (head + u) % RING)
            for g in range(head + loops * RING, tail):
                body(g, g // RING, g % RING)

        @block.sync
        def _(sp):
            def load(g, r, b):
                wait(sp, folded, g * FOLDS + (1 - 3) * FOLDS)
                for k in range(H + 1):
                    sp.dma_start(flags[b][k * G:(k + 1) * G, :],
                                 flag_rows[bass.ds(g * G, G), :]).then_inc(control[b], 16)
                sp.dma_start(offs[b][0:1, :].rearrange("p (w s) -> p w s", w=2),
                             tile_offsets[:, bass.ds(g * G, SLOT)].rearrange("(p w) s -> p w s", p=1)
                             ).then_inc(control[b], 16)

            over_groups(sp, load, 3, GROUPS)
        CONTROL = 16 * (H + 2)

        @block.gpsimd
        def _(pool):
            def gather(g, r, b):
                wait(pool, summed, (g - RING) * (G // 2) + G // 2)
                nc.gpsimd.tensor_copy(idx[b], m["srcs"][:, bass.ds(g * G, G)]).then_inc(idx_ready, 1)
                hold(pool, idx_ready, g + 1, passed)
                for s in range(G):
                    nc.gpsimd.indirect_dma_start(
                        out=xg[b][:, s, 0:D], out_offset=None, in_=xl_table,
                        in_offset=bass.IndirectOffsetOnAxis(ap=idx[b][:, s:s + 1], axis=0)
                    ).then_inc(gathered[b], 16)

            over_groups(pool, gather, 3, GROUPS)

        @block.tensor
        def _(pe):
            ident = m["ident"]

            def turn_sel(g, b, q):
                n = g * NQ + q
                pe.wait_ge(sel_built, n + 1)
                wait(pe, selT_made, n - 1)
                for k in range(Q):
                    i = nc.tensor.transpose(t_ps[q % 2][:, k * P:(k + 1) * P], sel[b][:, q * Q + k, :], ident[:, :])
                i.then_inc(selT_turned, 1)

            def sum_z(g, r, b, q, tiles):
                n = g * NQ + q
                if q == 0:
                    pe.wait_ge(gathered[b], r * (16 * G) + 16 * G)
                pe.wait_ge(selT_made, n + 1)
                wait(pe, z_rect, n - 1)
                for k in range(Q):
                    s = q * Q + k
                    zs = z_ps[q % 2][:, k * P:(k + 1) * P]
                    nc.tensor.matmul(zs, xg[b][:, s, 0:D], ident[:, :], start=True, stop=False)
                    for i in range(3):
                        last_i = nc.tensor.matmul(zs, m["xr3"][:, bass.ds(tiles[s] + i * D, D)], selT[b][:, s, :],
                                                  start=False, stop=(i == 2))
                last_i.then_inc(z_summed, 1)

            def score(g, q):
                n = g * NQ + q
                pe.wait_ge(z_rect, n + 1)
                if q == 0:
                    wait(pe, scores_kept, g)
                for k in range(Q):
                    s = q * Q + k
                    i = nc.tensor.matmul(score_ps[:, s:G * H:G], z[q % 2][:, k * P:(k + 1) * P], m["att"][:, :],
                                         start=True, stop=True)
                i.then_inc(z_scored, 1)

            def weigh(g, b):
                for p in range(G // 2):
                    n = g * (G // 2) + p
                    if p % 2 == 0:
                        pe.wait_ge(messages, g * NQ + (p // 2 + 1))
                    wait(pe, folded, g * FOLDS + (2 * p - 1) if p >= 2 else (g - 1) * FOLDS + (G - 1 + 2 * p))
                    for s in (2 * p, 2 * p + 1):
                        i = nc.tensor.matmul(o_ps[p % 2][:, (s % 2) * W:(s % 2 + 1) * W], sel[b][:, s, :],
                                             xg[b][:, s, :], start=True, stop=True)
                    i.then_inc(summed, 1)

            def body(g, r, b, new=True, old=True):
                h, c = g - 1, (b + RING - 1) % RING
                if new:
                    hold(pe, control[b], r * CONTROL + CONTROL, passed)
                    _, tiles = nc.values_load_multi_w_load_instructions(
                        offs[b][0:1, 1:SLOT], engines=(PE,), min_val=0, max_val=(TILES - 1) * 3 * D,
                        skip_runtime_bounds_check_because="the tile is held below TILES")
                if old:
                    hold(pe, scores_kept, h + 1, passed)
                    nc.tensor.transpose(turned_ps[0:G * H, :], scores, ident[:, :]).then_inc(turned, 1)
                if new:
                    turn_sel(g, b, 0)
                    turn_sel(g, b, 1)
                    sum_z(g, r, b, 0, tiles)
                if old:
                    pe.wait_ge(last_made, h + 1)
                    nc.tensor.transpose(lastT_ps, last[0:G * (H + 1), :], ident[0:G * (H + 1), 0:G * (H + 1)]
                                        ).then_inc(last_turned, 1)
                if new:
                    turn_sel(g, b, 2)
                    sum_z(g, r, b, 1, tiles)
                    score(g, 0)
                if old:
                    pe.wait_ge(last_kept, h + 1)
                    for s in range(G):
                        i = nc.tensor.matmul(found_ps[:, s, :], sel[c][:, s, :], lastT[:, s:G * (H + 1):G],
                                             start=True, stop=True)
                    i.then_inc(found_made, 1)
                if new:
                    turn_sel(g, b, 3)
                    sum_z(g, r, b, 2, tiles)
                    score(g, 1)
                if old:
                    pe.wait_ge(mx_made, h + 1)
                    for s in range(G):
                        i = nc.tensor.matmul(mx_ps[:, s * 3 * H:(s + 1) * 3 * H], selT[c][:, s, :],
                                             mx3[:, s * 3 * H:(s + 1) * 3 * H], start=True, stop=True)
                    i.then_inc(mx_picked, 1)
                if new:
                    sum_z(g, r, b, 3, tiles)
                    score(g, 2)
                    score(g, 3)
                if old:
                    weigh(h, c)

            body(0, 0, 0, old=False)
            body(1, 0, 1)
            with pe.Fori(0, (GROUPS - 2) // RING) as it:
                for u in range(RING):
                    body(it * RING + (2 + u), it + (2 + u) // RING, (2 + u) % RING)
            body(GROUPS, GROUPS // RING, GROUPS % RING, new=False)

        @block.scalar
        def _(act):
            def keep_selT(g, b, q):
                act.wait_ge(selT_turned, g * NQ + (q + 1))
                nc.scalar.copy(selT[b][:, q * Q:(q + 1) * Q, :],
                               t_ps[q % 2][:, :].rearrange("p (s e) -> p s e", s=Q)).then_inc(selT_made, 1)

            def scale_z(g, q):
                n = g * NQ + q
                act.wait_ge(z_summed, n + 1)
                wait(act, z_scored, n - 1)
                nc.scalar.activation(z[q % 2], z_ps[q % 2][:, :], ACT.Copy, scale=SLOPE).then_inc(z_scaled, 1)

            def body(g, r, b, new=True, old=True):
                h, c = g - 1, (b + RING - 1) % RING
                if new:
                    keep_selT(g, b, 0)
                    keep_selT(g, b, 1)
                    scale_z(g, 0)
                if old:
                    act.wait_ge(last_turned, h + 1)
                    nc.scalar.copy(lastT, lastT_ps).then_inc(last_kept, 1)
                if new:
                    keep_selT(g, b, 2)
                    scale_z(g, 1)
                    keep_selT(g, b, 3)
                    scale_z(g, 2)
                if old:
                    act.wait_ge(grow_in, h + 1)
                    nc.scalar.activation(grow[:, H:2 * H], grow[:, 0:H], ACT.Exp).then_inc(grown, 1)
                if new:
                    scale_z(g, 3)
                if old:
                    act.wait_ge(diff_made, h + 1)
                    nc.scalar.activation(xg[c][:, :, D:W], diff.rearrange("p (s h) -> p s h", h=H),
                                         ACT.Exp).then_inc(weights, 1)
                if new:
                    act.wait_ge(z_scored, g * NQ + NQ)
                    nc.scalar.copy(scores, score_ps[:, 0:G * H]).then_inc(scores_kept, 1)

            body(0, 0, 0, old=False)
            body(1, 0, 1)
            with act.Fori(0, (GROUPS - 2) // RING) as it:
                for u in range(RING):
                    body(it * RING + (2 + u), it + (2 + u) // RING, (2 + u) % RING)
            body(GROUPS, GROUPS // RING, GROUPS % RING, new=False)

        @block.vector
        def _(dve):
            found3 = found.rearrange("p (h s) -> p h s", s=SLOT)
            upmax3 = upmax.rearrange("p (h s) -> p h s", s=SLOT)
            reset3 = reset[:, 0:H * SLOT].rearrange("p (h s) -> p h s", s=SLOT)
            mx4 = mx3.rearrange("p (s i h) -> p i h s", i=3, h=H)
            rest3 = rest.rearrange("p (h s) -> p h s", s=G)

            def build_sel(g, b, q):
                d = m["dloc"][:, bass.ds(g * G + q * Q, Q)].unsqueeze(2).to_broadcast([P, Q, P])
                i = m["iota_row"][:, :].unsqueeze(1).to_broadcast([P, Q, P])
                nc.vector.tensor_tensor(sel[b][:, q * Q:(q + 1) * Q, :], i, d, ALU.is_equal).then_inc(sel_built, 1)

            def rectify(g, q):
                dve.wait_ge(z_scaled, g * NQ + (q + 1))
                nc.vector.tensor_tensor(z[q % 2], z_ps[q % 2][:, :], z[q % 2], ALU.max).then_inc(z_rect, 1)

            def body(g, r, b, new=True, old=True):
                h, c = g - 1, (b + RING - 1) % RING
                done = [0]

                def link(ins):
                    done[0] += 1
                    ins.then_inc(chain, 1)
                    dve.wait_ge(chain, h * CHAIN + done[0])

                if old:
                    link(nc.vector.tensor_copy(
                        reset3[:, :, 1:SLOT],
                        r0[:, bass.ds(h * G, G)].unsqueeze(1).to_broadcast([P, H, G])))
                    dve.wait_ge(control[c], (r if c < b else r - 1) * CONTROL + CONTROL)
                    dve.wait_ge(turned, h + 1)
                    link(nc.vector.tensor_tensor_scan(running[0:G * H, :], flags[c][0:G * H, 0:P],
                                                      turned_ps[0:G * H, :], RESET, ALU.add, ALU.max))
                    nc.vector.tensor_tensor(last[0:G * (H + 1), :], running[0:G * (H + 1), :],
                                            flags[c][0:G * (H + 1), P:2 * P], ALU.mult).then_inc(last_made, 1)
                if new:
                    rectify(g, 0)
                    rectify(g, 1)
                if old:
                    dve.wait_ge(found_made, h + 1)
                    link(nc.vector.tensor_scalar(absent, found_ps[:, :, H], BIG, -BIG, ALU.mult, ALU.add))
                    link(nc.vector.tensor_tensor(found3[:, :, 1:SLOT],
                                                 found_ps[:, :, 0:H].rearrange("p s h -> p h s"),
                                                 absent.unsqueeze(1).to_broadcast([P, H, G]), ALU.add))
                    link(nc.vector.tensor_tensor_scan(upto, reset[:, 0:H * SLOT], found, RESET, ALU.add, ALU.max))
                    link(nc.vector.tensor_tensor_scan(upmax[:, ::-1], reset[:, 1:H * SLOT + 1][:, ::-1],
                                                      upto[:, ::-1], RESET, ALU.add, ALU.max))
                    nc.vector.tensor_tensor(grow[:, 0:H], found3[:, :, 0], upmax3[:, :, 0],
                                            ALU.subtract).then_inc(grow_in, 1)
                    link(nc.vector.tensor_copy(mx4[:, 0], upmax3[:, :, 1:SLOT]))
                    link(nc.vector.tensor_tensor(rest3, upmax3[:, :, 1:SLOT], mx4[:, 0], ALU.subtract))
                    link(nc.vector.tensor_copy(mx4[:, 1], rest3))
                    nc.vector.tensor_tensor(mx4[:, 2], rest3, mx4[:, 1], ALU.subtract).then_inc(mx_made, 1)
                    dve.wait_ge(grow_in, h + 1)
                    link(nc.vector.tensor_copy(found3[:, :, 0], upmax3[:, :, G]))
                if new:
                    rectify(g, 2)
                    rectify(g, 3)
                if old:
                    dve.wait_ge(mx_picked, h + 1)
                    link(nc.vector.tensor_reduce(
                        mx.rearrange("p (s h) -> p s h", h=H),
                        mx_ps.rearrange("p (s i h) -> p s h i", i=3, h=H), axis=AX_X, op=ALU.add))
                    link(nc.vector.tensor_tensor(
                        diff.rearrange("p (s h) -> p s h", h=H), scores.rearrange("p (h s) -> p s h", h=H),
                        mx.rearrange("p (s h) -> p s h", h=H), ALU.subtract))
                    nc.vector.tensor_scalar(diff, diff, 0.0, None, ALU.min).then_inc(diff_made, 1)
                    _, tiles = nc.values_load_multi_w_load_instructions(
                        offs[c][0:1, SLOT:2 * SLOT], engines=(DVE,), min_val=0, max_val=(TILES - 1) * W,
                        skip_runtime_bounds_check_because="the tile is held below TILES")
                    dve.wait_ge(grown, h + 1)
                    wait(dve, folded, h * FOLDS)
                    carried = m["sums"][:, bass.ds(tiles[0], W)]
                    msg4 = carried[:, 0:D].rearrange("p (h c) -> p h c", h=H)
                    nc.vector.tensor_tensor(msg4, msg4, grow[:, H:2 * H].unsqueeze(2).to_broadcast([P, H, C]),
                                            ALU.mult).then_inc(chain, 1)
                    done[0] += 1
                    nc.vector.tensor_tensor(carried[:, D:W], carried[:, D:W], grow[:, H:2 * H],
                                            ALU.mult).then_inc(folded, 1)
                    dve.wait_ge(weights, h + 1)
                    for q in range(NQ):
                        x4 = xg[c][:, q * Q:(q + 1) * Q, 0:D].rearrange("p s (h c) -> p s h c", h=H)
                        nc.vector.tensor_tensor(
                            x4, x4, xg[c][:, q * Q:(q + 1) * Q, D:W].unsqueeze(3).to_broadcast([P, Q, H, C]),
                            ALU.mult).then_inc(messages, 1)
                    dve.wait_ge(chain, h * CHAIN + done[0])
                for s in range(G):
                    if old:
                        if s % 2 == 0:
                            dve.wait_ge(summed, h * (G // 2) + (s // 2 + 1))
                        dve.wait_ge(folded, h * FOLDS + (s + 1))
                        to = m["sums"][:, bass.ds(tiles[s + 1], W)]
                        nc.vector.tensor_tensor(to, to, o_ps[(s // 2) % 2][:, (s % 2) * W:(s % 2 + 1) * W],
                                                ALU.add).then_inc(folded, 1)
                    if new and s % Q == Q - 1:
                        build_sel(g + 1, (b + 1) % RING, s // Q)
                assert not old or done[0] == CHAIN, done[0]

            nc.vector.memset(m["sums"][:, :], 0.0).then_inc(zeroed, 1)
            nc.vector.memset(found, -BIG).then_inc(zeroed, 1)
            nc.vector.memset(running, 1.0).then_inc(zeroed, 1)
            nc.vector.memset(reset, RESET).then_inc(zeroed, 1)
            for q in range(NQ):
                build_sel(0, 0, q)
            dve.wait_ge(zeroed, 4)
            body(0, 0, 0, old=False)
            body(1, 0, 1)
            with dve.Fori(0, (GROUPS - 2) // RING) as it:
                for u in range(RING):
                    body(it * RING + (2 + u), it + (2 + u) // RING, (2 + u) % RING)
            body(GROUPS, GROUPS // RING, GROUPS % RING, new=False)


def dense(nc, a, m, layer, xl_table, out):
    final = out is not None
    ctx = ExitStack()
    with ctx:
        def sem(name):
            return ctx.enter_context(nc.semaphore(f"d{layer}_{name}"))

        area = Area(m["work"])
        B = BT * P
        h = area.take(B)
        hT = area.take(B)
        u = area.take(FB * Q * P).rearrange("p (f n) -> p f n", f=FB)
        y = area.take(B)
        yT = area.take(B)
        xres = area.take(B)
        both = area.take(BT * 2 * D)
        w1 = area.take(F)
        w2 = area.take(F).rearrange("p (f d) -> p f d", f=FB)
        b1 = area.take(FB)
        rows = area.take(4 * D).rearrange("p (k d) -> p k d", k=4)
        den = area.take(BT * H)
        stats = area.take(BT * 6)
        norm = area.take(BT * 2)
        dev = area.take(BT)
        eps = area.take(1)
        turn_ps = [ctx.enter_context(nc.psum_tensor(f"d{layer}_t{i}", [P, 512], F32)) for i in range(2)]
        u_ps = [ctx.enter_context(nc.psum_tensor(f"d{layer}_u{i}", [P, 512], F32)) for i in range(FB)]
        y_ps = [ctx.enter_context(nc.psum_tensor(f"d{layer}_y{i}", [P, 512], F32)) for i in range(2)]
        HALVES = ((0, Q), (Q, BT))

        names = ("weights_in", "x_in", "h_made", "h_turned", "hT_kept", "u_made", "u_kept", "y_made", "y_added",
                 "chain", "var_made", "dev_made", "normed", "y_turned", "yT_kept", "projected", "added",
                 "hi", "rest1", "mid", "low", "stored", "att0", "passed", "y_free")
        (weights_in, x_in, h_made, h_turned, hT_kept, u_made, u_kept, y_made, y_added, chain, var_made, dev_made,
         normed, y_turned, yT_kept, projected, added, hi, rest1, mid, low, stored, att0, passed, y_free) = (sem(s) for s in names)
        CHAIN = 3 + 3 + 4 + (3 if final else 0)
        NORMS = 2 if final else 1
        LOADS = 16 * 7
        block = ctx.enter_context(nc.Block())
        x3 = parts_view(m)
        sums3 = m["sums"][:, :].rearrange("p (t w) -> p t w", w=W)
        f_, l_ = f"f{layer}_", f"ln{layer}_"

        def rows_of(dram, k):
            return dram[bass.ds(k * B, B), :].rearrange("(t p) d -> p t d", p=P)

        @block.sync
        def _(sp):
            sp.dma_start(w1, a[f_ + "w1"]).then_inc(weights_in, 16)
            sp.dma_start(w2, a[f_ + "w2"].rearrange("(f p) d -> p f d", p=P)).then_inc(weights_in, 16)
            sp.dma_start(b1, a[f_ + "b1"]).then_inc(weights_in, 16)
            for k, name in enumerate((f"c{layer}_bias", f_ + "b2", l_ + "g", l_ + "b")):
                sp.dma_start(rows[:, k, :], a[name].partition_broadcast(P)).then_inc(weights_in, 16)
            if not final:
                load_projection(sp, a, m, 2, weights_in)
            else:
                with sp.Fori(0, BATCHES) as k:
                    sp.wait_ge(h_made, k + 1)
                    sp.dma_start(xres.rearrange("p (t d) -> p t d", t=BT), rows_of(a["x"], k)).then_inc(x_in, 16)

        @block.gpsimd
        def _(pool):
            with pool.Fori(0, BATCHES) as k:
                if final:
                    pool.wait_ge(normed, k * NORMS + NORMS)
                    pool.dma_start(rows_of(out, k), y.rearrange("p (t d) -> p t d", t=BT)).then_inc(stored, 16)
                else:
                    pool.wait_ge(added, k * BT + BT)
                    pool.dma_start(rows_of(xl_table, k),
                                   both.rearrange("p (t d) -> p t d", t=BT)[:, :, 0:D]).then_inc(stored, 16)
                pool.wait_ge(stored, k * 16 + 16)
                pool.sem_inc(y_free, 1)

        @block.tensor
        def _(pe):
            ident = m["ident"][:, :]
            pe.wait_ge(weights_in, LOADS + (0 if final else 16 * (4 + H)))

            def turn(src, done):
                for n, (lo, hi_) in enumerate(HALVES):
                    for j in range(lo, hi_):
                        i = nc.tensor.transpose(turn_ps[n][:, (j - lo) * P:(j - lo + 1) * P],
                                                src[:, j * P:(j + 1) * P], ident)
                    i.then_inc(done, 1)

            with pe.Fori(0, BATCHES) as k:
                pe.wait_ge(h_made, k + 1)
                turn(h, h_turned)
                for n, (lo, hi_) in enumerate(HALVES):
                    cols = slice(lo * P, hi_ * P)
                    pe.wait_ge(hT_kept, k * 2 + (n + 1))
                    for f in range(FB):
                        if n:
                            pe.wait_ge(u_kept, k * 2 * FB + (f + 1))
                        nc.tensor.matmul(u_ps[f][:, 0:(hi_ - lo) * P], w1[:, f * P:(f + 1) * P], hT[:, cols],
                                         start=True, stop=True).then_inc(u_made, 1)
                    pe.wait_ge(u_kept, k * 2 * FB + (n * FB + FB))
                    for j in range(lo, hi_):
                        at = slice((j - lo) * P, (j - lo + 1) * P)
                        for f in range(FB):
                            i = nc.tensor.matmul(y_ps[n][:, at], u[:, f, at], w2[:, f, :],
                                                 start=(f == 0), stop=(f == FB - 1))
                    i.then_inc(y_made, 1)
                if not final:
                    pe.wait_ge(normed, k + 1)
                    turn(y, y_turned)
                    pe.wait_ge(yT_kept, k * 2 + 2)
                    for j in range(BT):
                        i = nc.tensor.matmul(u_ps[j % FB][:, (j // FB) * 2 * D:(j // FB + 1) * 2 * D],
                                             yT[:, j * P:(j + 1) * P], m["wproj"][:, :], start=True, stop=True)
                    i.then_inc(projected, 1)

        @block.scalar
        def _(act):
            act.wait_ge(weights_in, LOADS + (0 if final else 16 * (4 + H)))
            with act.Fori(0, BATCHES) as k:
                for n, (lo, hi_) in enumerate(HALVES):
                    act.wait_ge(h_turned, k * 2 + (n + 1))
                    nc.scalar.copy(hT[:, lo * P:hi_ * P], turn_ps[n][:, 0:(hi_ - lo) * P]).then_inc(hT_kept, 1)
                for n, (lo, hi_) in enumerate(HALVES):
                    if n:
                        act.wait_ge(y_made, k * 2 + 1)
                    for f in range(FB):
                        act.wait_ge(u_made, k * 2 * FB + (n * FB + f + 1))
                        nc.scalar.activation(u[:, f, 0:(hi_ - lo) * P], u_ps[f][:, 0:(hi_ - lo) * P], ACT.Relu,
                                             bias=b1[:, f:f + 1]).then_inc(u_kept, 1)
                for r in range(NORMS):
                    act.wait_ge(var_made, k * NORMS + (r + 1))
                    nc.scalar.activation(dev, norm[:, 1:2 * BT:2], ACT.Sqrt, bias=eps).then_inc(dev_made, 1)
                if not final:
                    for n, (lo, hi_) in enumerate(HALVES):
                        act.wait_ge(y_turned, k * 2 + (n + 1))
                        nc.scalar.copy(yT[:, lo * P:hi_ * P], turn_ps[n][:, 0:(hi_ - lo) * P]).then_inc(yT_kept, 1)
                    rest = both.rearrange("p (t d) -> p t d", t=BT)[:, :, D:2 * D]
                    tiles = bass.ds(k * BT, BT)
                    act.wait_ge(added, k * BT + BT)
                    nc.scalar.copy(x3[:, tiles, 0, :], rest).then_inc(hi, 1)
                    act.wait_ge(rest1, k + 1)
                    nc.scalar.copy(x3[:, tiles, 1, :], rest).then_inc(mid, 1)

        @block.vector
        def _(dve):
            nc.vector.memset(eps, EPS).then_inc(att0, 1)
            dve.sem_inc(y_free, 1)
            dve.wait_ge(att0, 1)
            dve.wait_ge(weights_in, LOADS + (0 if final else 16 * (4 + H)))
            h3 = h.rearrange("p (t d) -> p t d", t=BT)
            y3 = y.rearrange("p (t d) -> p t d", t=BT)
            norm3 = norm.rearrange("p (t k) -> p t k", k=2)

            def all_tiles(k):
                return rows[:, k, :].unsqueeze(1).to_broadcast([P, BT, D])

            with dve.Fori(0, BATCHES) as k:
                done = [0]

                def link(ins):
                    done[0] += 1
                    ins.then_inc(chain, 1)
                    dve.wait_ge(chain, k * CHAIN + done[0])

                def normalize(r, affine):
                    for j in range(BT):
                        i = nc.vector.bn_stats(stats[:, j * 6:(j + 1) * 6], y3[:, j, :])
                    link(i)
                    dve.sem_inc(passed, 1)
                    for j in range(BT - 1):
                        nc.vector.bn_aggr(norm3[:, j, :], stats[:, j * 6:(j + 1) * 6])
                    nc.vector.bn_aggr(norm3[:, BT - 1, :], stats[:, (BT - 1) * 6:BT * 6]).then_inc(var_made, 1)
                    dve.wait_ge(var_made, k * NORMS + (r + 1))
                    dve.wait_ge(dev_made, k * NORMS + (r + 1))
                    link(nc.vector.reciprocal(dev, dev))
                    for j in range(BT):
                        ins = nc.vector.tensor_scalar(y3[:, j, :], y3[:, j, :], norm3[:, j, 0:1], dev[:, j:j + 1],
                                                      ALU.subtract, ALU.mult)
                    if not affine:
                        ins.then_inc(normed, 1)
                    else:
                        link(ins)
                        link(nc.vector.tensor_tensor(y3, y3, all_tiles(2), ALU.mult))
                        nc.vector.tensor_tensor(y3, y3, all_tiles(3), ALU.add).then_inc(normed, 1)

                sums = sums3[:, bass.ds(k * BT, BT), :]
                den3 = den.rearrange("p (t h) -> p t h", h=H)
                link(nc.vector.tensor_scalar(den3, sums[:, :, D:W], 1e-16, None, ALU.add))
                link(nc.vector.reciprocal(den, den))
                link(nc.vector.tensor_tensor(
                    h.rearrange("p (t h c) -> p t h c", t=BT, h=H),
                    sums[:, :, 0:D].rearrange("p t (h c) -> p t h c", h=H),
                    den3.unsqueeze(3).to_broadcast([P, BT, H, C]), ALU.mult))
                nc.vector.tensor_tensor(h3, h3, all_tiles(0), ALU.add).then_inc(h_made, 1)
                if final:
                    dve.wait_ge(y_free, k + 1)
                for n, (lo, hi_) in enumerate(HALVES):
                    dve.wait_ge(y_made, k * 2 + (n + 1))
                    link(nc.vector.tensor_tensor(y[:, lo * P:hi_ * P], y_ps[n][:, 0:(hi_ - lo) * P],
                                                 h[:, lo * P:hi_ * P], ALU.add))
                link(nc.vector.tensor_tensor(y3, y3, all_tiles(1), ALU.add))
                normalize(0, True)
                if final:
                    dve.wait_ge(normed, k * NORMS + 1)
                    dve.wait_ge(x_in, k * 16 + 16)
                    link(nc.vector.tensor_tensor(y, y, xres, ALU.add))
                    normalize(1, False)
                else:
                    dve.wait_ge(projected, k + 1)
                    b3 = both.rearrange("p (t d) -> p t d", t=BT)
                    for j in range(BT):
                        nc.vector.tensor_tensor(b3[:, j, :], u_ps[j % FB][:, (j // FB) * 2 * D:(j // FB + 1) * 2 * D],
                                                m["bproj"][:, :], ALU.add).then_inc(added, 1)
                    rest = b3[:, :, D:2 * D]
                    tiles = bass.ds(k * BT, BT)
                    dve.wait_ge(hi, k + 1)
                    nc.vector.tensor_tensor(rest, rest, x3[:, tiles, 0, :], ALU.subtract).then_inc(rest1, 1)
                    dve.wait_ge(mid, k + 1)
                    nc.vector.tensor_tensor(x3[:, tiles, 2, :], rest, x3[:, tiles, 1, :], ALU.subtract).then_inc(low, 1)
                    dve.wait_ge(low, k + 1)
                    dve.wait_ge(stored, k * 16 + 16)
                assert done[0] == CHAIN, (done[0], CHAIN)


def kernel(**inputs):
    import numpy as np
    import concourse.bacc as bacc
    from concourse.bass_utils import run_bass_kernel_spmd

    given = {k.removeprefix("L0_gnn_"): np.asarray(v) for k, v in inputs.items()}
    x = np.zeros((NP, D), np.float32)
    x[:N] = given["x"]
    src = np.zeros(((CHUNKS + 1) * P,), np.int32)
    dst = np.full(((CHUNKS + 1) * P,), NP - 1, np.int32)
    src[:E], dst[:E] = given["src"], given["dst"]
    src, dst = src.reshape(-1, P), dst.reshape(-1, P)
    arrays = {"x": x, "xT": np.ascontiguousarray(x.T), "src_chunks": src, "dst_chunks": dst,
              "last_dst": np.ascontiguousarray(dst[:CHUNKS, P - 1])}
    for k, v in given.items():
        if k in ("x", "src", "dst"):
            continue
        if k.endswith("_att"):
            v = v.reshape(H * C, 1)
        elif k.endswith("_b1"):
            v = np.ascontiguousarray(v.reshape(FB, P).T)
        arrays[k] = v

    nc = bacc.Bacc("TRN2", target_bir_lowering=False, num_devices=1)
    a = {k: nc.dram_tensor("in_" + k, v.shape, mybir.dt.from_np(v.dtype), kind="ExternalInput").ap()
         for k, v in arrays.items()}
    out = nc.dram_tensor("out", [NP, D], F32, kind="ExternalOutput").ap()
    build(nc, a, out)
    r = run_bass_kernel_spmd(nc, [{"in_" + k: v for k, v in arrays.items()}], core_ids=[0])
    return r.results[0]["out"][:N]
```

```python
from contextlib import ExitStack

import concourse.bass as bass
from concourse import mybir

F32 = mybir.dt.float32
BF16 = mybir.dt.bfloat16
I32 = mybir.dt.int32
I16 = mybir.dt.int16
ALU = mybir.AluOpType
ACT = mybir.ActivationFunctionType
AX_X = mybir.AxisListType.X
DVE = mybir.EngineType.DVE
PE = mybir.EngineType.PE

P = 128
N = 12500
D = 128
H, C = 4, 32
F = 512
E = 200000
TILES = -(-N // P)
NP = TILES * P
CHUNKS = -(-E // P)
G = 16
SB = 13
STEPS = SB * P
GROUPS = STEPS // G
Q = 4
NQ = G // Q
W = D + H
RING = 3
BIG = 1.0e30
RESET = -1.0e38
EPS = 1e-5
SLOPE = 0.2
SLOT = G + 1
BT = 7
BATCHES = TILES // BT
FB = F // P
assert STEPS >= CHUNKS + TILES - 1 and GROUPS * G == STEPS and BATCHES * BT == TILES


def wait(eng, sem, value):
    if isinstance(value, int) and value <= 0:
        return
    eng.wait_ge(sem, value)


def hold(eng, sem, value, passed):
    wait(eng, sem, value)
    eng.sem_inc(passed, 1)


def build(nc, a, out):
    top = ExitStack()
    with top:
        def sb(name, shape, dt):
            return top.enter_context(nc.sbuf_tensor(name, shape, dt))

        def sem(name):
            return top.enter_context(nc.semaphore(name))

        xl_table = nc.dram_tensor("xl_table", [NP, D], F32).ap()
        flag_rows = nc.dram_tensor("flag_rows", [STEPS, 2 * P], BF16).ap()
        tile_of_step = nc.dram_tensor("tile_of_step", [SB, P], F32).ap()
        tile_offsets = nc.dram_tensor("tile_offsets", [2, STEPS + 1], I32).ap()

        m = {}
        m["xr3"] = sb("xr3", [P, TILES * 3 * D], BF16)
        m["sums"] = sb("sums", [P, TILES * W], F32)
        m["srcs"] = sb("srcs", [P, STEPS + 2 * G], I16)
        m["dloc"] = sb("dloc", [P, STEPS], BF16)
        m["resets"] = sb("resets", [P, STEPS], BF16)
        m["ident"] = sb("ident", [P, P], F32)
        m["ident16"] = sb("ident16", [P, P], BF16)
        m["iota_row"] = sb("iota_row", [P, P], BF16)
        m["wproj"] = sb("wproj", [P, 2 * D], F32)
        m["bproj"] = sb("bproj", [P, 2 * D], F32)
        m["att"] = sb("att", [P, G * H + G - 1], F32)
        WORK = 72384
        m["work"] = sb("work", [P, WORK // 4], F32)

        prepare(nc, a, m, flag_rows, tile_of_step, tile_offsets)
        project_input(nc, a, m, xl_table)
        edges(nc, a, m, 1, xl_table, flag_rows, tile_offsets)
        dense(nc, a, m, 1, xl_table, None)
        edges(nc, a, m, 2, xl_table, flag_rows, tile_offsets)
        dense(nc, a, m, 2, None, out)


class Area:

    def __init__(self, work):
        self.work, self.at = work, 0

    def take(self, columns, dt=F32):
        size = {F32: 4, I32: 4, BF16: 2, I16: 2}[dt]
        words = -(-columns * size // 4)
        v = self.work[:, self.at:self.at + words]
        self.at += words
        assert self.at <= self.work.shape[1], self.at
        return v if dt == F32 else v.bitcast(dt)[:, 0:columns]


def prepare(nc, a, m, flag_rows, tile_of_step, tile_offsets):
    ctx = ExitStack()
    with ctx:
        def sem(name):
            return ctx.enter_context(nc.semaphore("p_" + name))

        area = Area(m["work"])
        last_dst = area.take(CHUNKS, I32)
        end_tile = area.take(CHUNKS, I32)
        chunk_no = area.take(CHUNKS, I32)
        end_step = area.take(CHUNKS)
        chunk_f = area.take(CHUNKS)
        before = area.take(CHUNKS)
        step_i = area.take(SB, I32)
        step_no = area.take(SB)
        chunk_of = area.take(SB)
        tile_of = area.take(SB)
        tile_base = area.take(SB)
        chunk_idx = area.take(SB, I32)
        iota_i = area.take(P, I32)
        tcol = area.take(P)
        prep2 = area.at
        area2 = Area(m["work"])
        area2.at = prep2
        tiles_b = area.take(STEPS)
        trow = area.take(2 * (STEPS + 1), I32)
        src_i = m["sums"][:, 0:STEPS].bitcast(I32)
        dst_i = m["sums"][:, STEPS:2 * STEPS].bitcast(I32)
        src_f = m["sums"][:, 2 * STEPS:3 * STEPS]
        dst_f = m["sums"][:, 3 * STEPS:4 * STEPS]
        dloc_f = m["sums"][:, 4 * STEPS:5 * STEPS]
        flags = m["sums"][:, 5 * STEPS:6 * STEPS + STEPS].bitcast(BF16)[:, 0:2 * STEPS]
        ps = [ctx.enter_context(nc.psum_tensor(f"p_ps{i}", [P, 512], F32)) for i in range(2)]

        loaded, iotas, stair = sem("loaded"), sem("iotas"), sem("stair")
        ident0, gathered, tiles_out, tiles_in = sem("ident0"), sem("gathered"), sem("tiles_out"), sem("tiles_in")
        turned, moved, rows_out, flags_out, v = sem("turned"), sem("moved"), sem("rows_out"), sem("flags_out"), sem("v")
        tables, tT, tC = sem("tables"), sem("tT"), sem("tC")
        block = ctx.enter_context(nc.Block())

        @block.sync
        def _(sp):
            sp.dma_start(last_dst, a["last_dst"].partition_broadcast(P)).then_inc(loaded, 16)
            sp.wait_ge(tC, 1)
            sp.dma_start(tile_of_step, tcol[0:SB, :]).then_inc(tiles_out, 16)
            sp.wait_ge(tiles_out, 16)
            sp.dma_start(tiles_b, tile_of_step.rearrange("k p -> (k p)").partition_broadcast(P)).then_inc(tiles_in, 16)
            sp.wait_ge(rows_out, 1)
            sp.dma_start(tile_offsets.rearrange("a b -> (a b)").partition_broadcast(1), trow[0:1, :]).then_inc(flags_out, 16)
            sp.wait_ge(tables, 1)
            sp.dma_start(flag_rows.rearrange("(k p) f -> p k f", p=P),
                         flags.rearrange("p (k f) -> p k f", k=SB)).then_inc(flags_out, 16)
            sp.wait_ge(flags_out, 32)

        @block.gpsimd
        def _(pool):
            nc.gpsimd.iota(chunk_no, pattern=[[1, CHUNKS]], base=0, channel_multiplier=0).then_inc(iotas, 1)
            nc.gpsimd.iota(step_i, pattern=[[P, SB]], base=0, channel_multiplier=1).then_inc(iotas, 1)
            nc.gpsimd.iota(iota_i, pattern=[[1, P]], base=0, channel_multiplier=0).then_inc(iotas, 1)
            nc.gpsimd.memset(m["ident"][:, :], 0.0).then_inc(ident0, 1)
            pool.wait_ge(ident0, 1)
            nc.gpsimd.affine_select(out=m["ident"][:, :], in_=m["ident"][:, :], compare_op=ALU.not_equal,
                                    fill=1.0, base=0, pattern=[[-1, P]], channel_multiplier=1).then_inc(ident0, 1)
            pool.wait_ge(stair, 1)
            for k in range(SB):
                for rows, name in ((src_i, "src_chunks"), (dst_i, "dst_chunks")):
                    nc.gpsimd.indirect_dma_start(
                        out=rows[:, k * P:(k + 1) * P], out_offset=None, in_=a[name],
                        in_offset=bass.IndirectOffsetOnAxis(ap=chunk_idx[:, k:k + 1], axis=0)).then_inc(gathered, 16)
            pool.wait_ge(gathered, 32 * SB)

        @block.vector
        def _(dve):
            n = [0]

            def link(ins):
                n[0] += 1
                ins.then_inc(v, 1)
                dve.wait_ge(v, n[0])

            dve.wait_ge(ident0, 2)
            link(nc.vector.tensor_copy(m["ident16"][:, :], m["ident"][:, :]))
            dve.wait_ge(iotas, 3)
            link(nc.vector.tensor_copy(m["iota_row"][:, :], iota_i))
            link(nc.vector.memset(m["srcs"][:, STEPS:], 0))
            link(nc.vector.tensor_copy(step_no, step_i))
            link(nc.vector.tensor_copy(chunk_f, chunk_no))
            dve.wait_ge(loaded, 16)
            link(nc.vector.tensor_scalar(end_tile, last_dst, 7, None, ALU.arith_shift_right))
            link(nc.vector.tensor_copy(end_step, end_tile))
            link(nc.vector.tensor_tensor(end_step, end_step, chunk_f, ALU.add))
            for k in range(SB):
                link(nc.vector.tensor_scalar(before, end_step, step_no[:, k:k + 1], None, ALU.is_lt))
                link(nc.vector.tensor_reduce(chunk_of[:, k:k + 1], before, axis=AX_X, op=ALU.add))
            link(nc.vector.tensor_tensor(tile_of, step_no, chunk_of, ALU.subtract))
            link(nc.vector.tensor_scalar(tile_of, tile_of, float(TILES - 1), None, ALU.min))
            link(nc.vector.tensor_scalar(tile_base, tile_of, float(P), None, ALU.mult))
            nc.vector.tensor_copy(chunk_idx, chunk_of).then_inc(stair, 1)
            dve.wait_ge(tT, 1)
            nc.vector.tensor_copy(tcol[0:SB, :], ps[0][0:SB, 0:P]).then_inc(tC, 1)
            dve.wait_ge(tiles_in, 16)
            link(nc.vector.memset(m["resets"][:, 0:1], 0.0))
            link(nc.vector.tensor_tensor(m["resets"][:, 1:STEPS], tiles_b[:, 1:STEPS], tiles_b[:, 0:STEPS - 1],
                                         ALU.not_equal))
            link(nc.vector.tensor_scalar(m["resets"][:, :], m["resets"][:, :], RESET, None, ALU.mult))
            link(nc.vector.memset(trow[0:1, :], 0))
            link(nc.vector.tensor_scalar(trow[0:1, 1:STEPS + 1], tiles_b[0:1, :], float(3 * D), None, ALU.mult))
            nc.vector.tensor_scalar(trow[0:1, STEPS + 2:2 * STEPS + 2], tiles_b[0:1, :], float(W), None,
                                    ALU.mult).then_inc(rows_out, 1)
            dve.wait_ge(gathered, 32 * SB)
            link(nc.vector.tensor_copy(src_f, src_i))
            link(nc.vector.tensor_copy(dst_f, dst_i))
            for k in range(SB):
                c = slice(k * P, (k + 1) * P)
                link(nc.vector.tensor_scalar(dloc_f[:, c], dst_f[:, c], tile_base[:, k:k + 1], None, ALU.subtract))
            d3 = dst_f.rearrange("p (k e) -> p k e", k=SB)
            f4 = flags.rearrange("p (k w e) -> p k w e", k=SB, w=2)
            link(nc.vector.tensor_tensor(f4[:, :, 0, 1:P], d3[:, :, 1:P], d3[:, :, 0:P - 1], ALU.not_equal))
            link(nc.vector.tensor_copy(f4[:, :, 1, 0:P - 1], f4[:, :, 0, 1:P]))
            link(nc.vector.memset(f4[:, :, 0, 0:1], 1.0))
            link(nc.vector.memset(f4[:, :, 1, P - 1:P], 1.0))
            nc.vector.tensor_scalar(f4[:, :, 0, :], f4[:, :, 0, :], RESET, None, ALU.mult).then_inc(tables, 1)
            nc.vector.tensor_copy(dloc_f[:, 0:1], dloc_f[:, 0:1]).then_inc(turned, 1)
            for k in range(SB):
                dve.wait_ge(moved, k + 1)
                c = slice(k * P, (k + 1) * P)
                link(nc.vector.tensor_copy(m["srcs"][:, c], ps[k % 2][:, 0:P]))
                nc.vector.tensor_copy(m["dloc"][:, c], ps[k % 2][:, P:2 * P]).then_inc(turned, 1)

        @block.tensor
        def _(pe):
            pe.wait_ge(ident0, 2)
            pe.wait_ge(stair, 1)
            nc.tensor.transpose(ps[0][0:SB, 0:P], tile_of, m["ident"][:, :]).then_inc(tT, 1)
            pe.wait_ge(tC, 1)
            for k in range(SB):
                pe.wait_ge(turned, max(1, k))
                c = slice(k * P, (k + 1) * P)
                nc.tensor.transpose(ps[k % 2][:, 0:P], src_f[:, c], m["ident"][:, :])
                nc.tensor.transpose(ps[k % 2][:, P:2 * P], dloc_f[:, c], m["ident"][:, :]).then_inc(moved, 1)


def load_projection(sp, a, m, layer, sem):
    c = f"c{layer}_"
    sp.dma_start(m["wproj"][:, 0:D], a[c + "wl"]).then_inc(sem, 16)
    sp.dma_start(m["wproj"][:, D:2 * D], a[c + "wr"]).then_inc(sem, 16)
    sp.dma_start(m["bproj"][:, 0:D], a[c + "bl"].partition_broadcast(P)).then_inc(sem, 16)
    sp.dma_start(m["bproj"][:, D:2 * D], a[c + "br"].partition_broadcast(P)).then_inc(sem, 16)
    for h in range(H):
        sp.dma_start(m["att"][h * C:(h + 1) * C, (h + 1) * G - 1:(h + 1) * G],
                     a[c + "att"][h * C:(h + 1) * C, :]).then_inc(sem, 16)
    return 16 * (4 + H)


def parts_view(m):
    return m["xr3"][:, :].rearrange("p (t i d) -> p t i d", i=3, d=D)


def project_input(nc, a, m, xl_table):
    ctx = ExitStack()
    with ctx:
        def sem(name):
            return ctx.enter_context(nc.semaphore("i_" + name))

        area = Area(m["work"])
        xT = [area.take(BT * P) for _ in range(2)]
        both = [area.take(BT * 2 * D) for _ in range(2)]
        ps = [ctx.enter_context(nc.psum_tensor(f"i_ps{i}", [P, 512], F32)) for i in range(2)]
        w_in, x_in, att0 = sem("w_in"), [sem("x_in0"), sem("x_in1")], sem("att0")
        made, added, hi, mid, rest1, low, stored, both_free = (
            sem(s) for s in ("made", "added", "hi", "mid", "rest1", "low", "stored", "both_free"))
        block = ctx.enter_context(nc.Block())
        x3 = parts_view(m)

        @block.sync
        def _(sp):
            sp.wait_ge(att0, 1)
            load_projection(sp, a, m, 1, w_in)
            with sp.Fori(0, BATCHES // 2) as it:
                for b in range(2):
                    k = it * 2 + b
                    sp.wait_ge(made, k * BT + BT)
                    sp.dma_start(xT[b], a["xT"][:, bass.ds(k * (BT * P), BT * P)]).then_inc(x_in[b], 16)

        @block.gpsimd
        def _(pool):
            nc.gpsimd.memset(m["att"][:, :], 0.0).then_inc(att0, 1)
            with pool.Fori(0, BATCHES // 2) as it:
                for b in range(2):
                    k = it * 2 + b
                    pool.wait_ge(added, k * BT + (BT + 2))
                    pool.dma_start(xl_table[bass.ds(k * (BT * P), BT * P), :].rearrange("(t p) d -> p t d", p=P),
                                   both[b].rearrange("p (t d) -> p t d", t=BT)[:, :, 0:D]).then_inc(stored, 16)
                    pool.wait_ge(stored, k * 16 + 16)
                    pool.sem_inc(both_free, 1)

        @block.tensor
        def _(pe):
            pe.sem_inc(made, 2 * BT)
            pe.wait_ge(w_in, 16 * (4 + H))
            with pe.Fori(0, BATCHES // 2) as it:
                for b in range(2):
                    k = it * 2 + b
                    pe.wait_ge(x_in[b], it * 16 + 16)
                    for j in range(BT):
                        pe.wait_ge(added, k * BT + (j + 1))
                        nc.tensor.matmul(ps[(b * BT + j) % 2][:, 0:2 * D], xT[b][:, j * P:(j + 1) * P],
                                         m["wproj"][:, :], start=True, stop=True).then_inc(made, 1)

        @block.vector
        def _(dve):
            dve.sem_inc(added, 2)
            dve.sem_inc(both_free, 2)
            dve.sem_inc(low, 2)
            with dve.Fori(0, BATCHES // 2) as it:
                for b in range(2):
                    k = it * 2 + b
                    b3 = both[b].rearrange("p (t d) -> p t d", t=BT)
                    for j in range(BT):
                        dve.wait_ge(made, k * BT + (j + 1 + 2 * BT))
                        if j == 0:
                            dve.wait_ge(both_free, k + 1)
                            dve.wait_ge(low, k + 1)
                        nc.vector.tensor_tensor(b3[:, j, :], ps[(b * BT + j) % 2][:, 0:2 * D], m["bproj"][:, :],
                                                ALU.add).then_inc(added, 1)
                    rest = b3[:, :, D:2 * D]
                    tiles = bass.ds(k * BT, BT)
                    dve.wait_ge(hi, k + 1)
                    nc.vector.tensor_tensor(rest, rest, x3[:, tiles, 0, :], ALU.subtract).then_inc(rest1, 1)
                    dve.wait_ge(mid, k + 1)
                    nc.vector.tensor_tensor(x3[:, tiles, 2, :], rest, x3[:, tiles, 1, :], ALU.subtract).then_inc(low, 1)

        @block.scalar
        def _(act):
            with act.Fori(0, BATCHES // 2) as it:
                for b in range(2):
                    k = it * 2 + b
                    rest = both[b].rearrange("p (t d) -> p t d", t=BT)[:, :, D:2 * D]
                    tiles = bass.ds(k * BT, BT)
                    act.wait_ge(added, k * BT + (BT + 2))
                    nc.scalar.copy(x3[:, tiles, 0, :], rest).then_inc(hi, 1)
                    act.wait_ge(rest1, k + 1)
                    nc.scalar.copy(x3[:, tiles, 1, :], rest).then_inc(mid, 1)


def edges(nc, a, m, layer, xl_table, flag_rows, tile_offsets):
    ctx = ExitStack()
    with ctx:
        sems = []

        def sem(name):
            sems.append(nc.alloc_semaphore(f"e{layer}_{name}"))
            return sems[-1]

        def pb(name):
            return ctx.enter_context(nc.psum_tensor(f"e{layer}_{name}", [P, 512], F32))

        area = Area(m["work"])
        xg = [area.take(G * W).rearrange("p (s w) -> p s w", s=G) for _ in range(RING)]
        sel = [area.take(G * P, BF16).rearrange("p (s n) -> p s n", s=G) for _ in range(RING)]
        selT = [area.take(G * P, BF16).rearrange("p (s e) -> p s e", s=G) for _ in range(RING)]
        sel32 = area.take(G * P).rearrange("p (s n) -> p s n", s=G)
        flags = [area.take(2 * P, BF16) for _ in range(RING)]
        idx = [area.take(G, I32) for _ in range(RING)]
        offs = [area.take(2 * SLOT, I32) for _ in range(RING)]
        z = [area.take(Q * P) for _ in range(2)]
        scores = area.take(P)
        running = area.take(P)
        last = area.take(P)
        last3 = area.take(G * 3 * (H + 1), BF16)
        lrest = area.take(G * (H + 1))
        seen = area.take(G * (H + 1))
        absent = area.take(G)
        found = area.take(H * SLOT)
        upto = area.take(H * SLOT)
        upmax = area.take(H * SLOT)
        reset = area.take(H * SLOT + 1)
        rest = area.take(H * G)
        mx3 = area.take(G * 3 * H, BF16)
        mx = area.take(G * H)
        diff = area.take(G * H)
        grow = area.take(2 * H)
        z_ps = [pb("z0"), pb("z1")]
        t_ps = ctx.enter_context(nc.psum_tensor(f"e{layer}_t", [P, 1024], BF16))
        score_ps, small_ps = pb("scores"), pb("small")
        o_ps = [pb("o0"), pb("o1"), pb("o2")]
        scoresT_ps = small_ps[:, 0:G * H]
        lastT_ps = small_ps[:, G * H:G * (2 * H + 1)]
        seen_ps = small_ps[:, G * (2 * H + 1):G * (2 * H + 1 + 3 * (H + 1))]
        mx_ps = small_ps[:, G * H:G * 4 * H]

        gathered = [[sem(f"gathered{b}_{q}") for q in range(NQ)] for b in range(RING)]
        control = [sem(f"control{b}") for b in range(RING)]
        idx_ready = sem("idx_ready")
        sel_built, selT_turned, selT_made = sem("sel_built"), sem("selT_turned"), sem("selT_made")
        z_summed, z_scaled, z_rect, z_scored = sem("z_summed"), sem("z_scaled"), sem("z_rect"), sem("z_scored")
        scores_kept, last_made, last_turned = sem("scores_kept"), sem("last_made"), sem("last_turned")
        last_split, sel32_made = sem("last_split"), sem("sel32_made")
        found_made, mx_made, mx_picked, chain = sem("found_made"), sem("mx_made"), sem("mx_picked"), sem("chain")
        grow_in, grown, diff_made, weights = sem("grow_in"), sem("grown"), sem("diff_made"), sem("weights")
        messages, summed, folded, zeroed = sem("messages"), sem("summed"), sem("folded"), sem("zeroed")
        passed, scanned, reset_made = sem("passed"), sem("scanned"), sem("reset_made")
        LEAD = 6
        CHAIN = 15
        FOLDS = G + 1
        block = ctx.enter_context(nc.Block())
        r0 = m["resets"]

        def over_groups(eng, body, head, tail):
            for g in range(head):
                body(g, g // RING, g % RING)
            loops = (tail - head) // RING
            with eng.Fori(0, loops) as it:
                for u in range(RING):
                    body(it * RING + (head + u), it + (head + u) // RING, (head + u) % RING)
            for g in range(head + loops * RING, tail):
                body(g, g // RING, g % RING)

        def over_iterations(eng, body):
            loops = (GROUPS - 3) // RING
            body(0, 0, 0, old=False)
            body(1, 0, 1)
            with eng.Fori(0, loops) as it:
                for u in range(RING):
                    body(it * RING + (2 + u), it + (2 + u) // RING, (2 + u) % RING)
            for g in range(2 + loops * RING, GROUPS):
                body(g, g // RING, g % RING, ahead=(g < GROUPS - 1))
            body(GROUPS, GROUPS // RING, GROUPS % RING, new=False, ahead=False)

        @block.sync
        def _(sp):
            def load(g, r, b):
                wait(sp, folded, g * FOLDS + (1 - 3) * FOLDS)
                for k in range(H + 1):
                    sp.dma_start(flags[b][k * G:(k + 1) * G, :],
                                 flag_rows[bass.ds(g * G, G), :]).then_inc(control[b], 16)
                sp.dma_start(offs[b][0:1, :].rearrange("p (w s) -> p w s", w=2),
                             tile_offsets[:, bass.ds(g * G, SLOT)].rearrange("(p w) s -> p w s", p=1)
                             ).then_inc(control[b], 16)

            over_groups(sp, load, 3, GROUPS)
        CONTROL = 16 * (H + 2)

        @block.gpsimd
        def _(pool):
            def gather(g, r, b):
                hold(pool, idx_ready, g + 1, passed)
                for s in range(G):
                    if s % Q == 0:
                        if not isinstance(g, int) or g >= RING:
                            hold(pool, summed, (g - RING) * (G // 2) + (s + Q) // 2, passed)
                    nc.gpsimd.indirect_dma_start(
                        out=xg[b][:, s, 0:D], out_offset=None, in_=xl_table,
                        in_offset=bass.IndirectOffsetOnAxis(ap=idx[b][:, s:s + 1], axis=0)
                    ).then_inc(gathered[b][s // Q], 16)

            over_groups(pool, gather, 3, GROUPS)

        @block.tensor
        def _(pe):
            ident = m["ident"]
            ident16 = m["ident16"]

            def turn_sel(g, b, half):
                n = g * 2 + half
                pe.wait_ge(sel_built, g * G + (half + 1) * (G // 2))
                wait(pe, selT_made, n)
                for k in range(G // 2):
                    i = nc.tensor.transpose(t_ps[:, k * P:(k + 1) * P], sel[b][:, half * (G // 2) + k, :],
                                            ident16[:, :])
                i.then_inc(selT_turned, 1)

            def sum_z(g, r, b, q, tiles):
                n = g * NQ + q
                hold(pe, gathered[b][q], r * (16 * Q) + 16 * Q, passed)
                pe.wait_ge(selT_made, g * 2 + (q // 2 + 1))
                wait(pe, z_rect, n - 1)
                for k in range(Q):
                    s = q * Q + k
                    zs = z_ps[q % 2][:, k * P:(k + 1) * P]
                    nc.tensor.matmul(zs, xg[b][:, s, 0:D], ident[:, :], is_transpose=True, start=True, stop=False)
                    for i in range(3):
                        last_i = nc.tensor.matmul(zs, m["xr3"][:, bass.ds(tiles[s % (G // 2)] + i * D, D)], selT[b][:, s, :],
                                                  start=False, stop=(i == 2))
                last_i.then_inc(z_summed, 1)

            def score(g, q):
                n = g * NQ + q
                pe.wait_ge(z_rect, n + 1)
                for k in range(Q):
                    s = q * Q + k
                    i = nc.tensor.matmul(score_ps[0:G * H, 0:P],
                                         m["att"][:, G - 1 - s:G - 1 - s + G * H], z[q % 2][:, k * P:(k + 1) * P],
                                         start=(s == 0), stop=(s == G - 1))
                i.then_inc(z_scored, 1)

            def weigh(g, b, p):
                pe.wait_ge(messages, g * G + (2 * p + 2))
                if p % 2 == 0:
                    pe.wait_ge(sel32_made, g * NQ + (p // 2 + 1))
                wait(pe, folded, g * FOLDS + (2 * p - 3) if p >= 3 else (g - 1) * FOLDS + (G - 3 + 2 * p))
                for s in (2 * p, 2 * p + 1):
                    i = nc.tensor.matmul(o_ps[(b * (G // 2) + p) % 3][:, (s % 2) * W:(s % 2 + 1) * W], sel32[:, s, :],
                                         xg[b][:, s, :], start=True, stop=True)
                i.then_inc(summed, 1)

            def load_tiles(g, r, b, half):
                hold(pe, control[b], r * CONTROL + CONTROL, passed)
                _, tiles = nc.values_load_multi_w_load_instructions(
                    offs[b][0:1, 1 + half * (G // 2):1 + (half + 1) * (G // 2)], engines=(PE,), min_val=0,
                    max_val=(TILES - 1) * 3 * D,
                    skip_runtime_bounds_check_because="the tile is held below TILES")
                return tiles

            def body(g, r, b, new=True, old=True, ahead=True):
                h, c = g - 1, (b + RING - 1) % RING
                g1, r1, b1 = g + 1, r + (b + 1) // RING, (b + 1) % RING
                if old:
                    pe.wait_ge(last_split, h + 1)
                    for s in range(G):
                        cols = slice(s * 3 * (H + 1), (s + 1) * 3 * (H + 1))
                        i = nc.tensor.matmul(seen_ps[:, cols], sel[c][:, s, :], last3[:, cols],
                                             start=True, stop=True)
                    i.then_inc(found_made, 1)
                if new:
                    tiles = load_tiles(g, r, b, 1)
                    sum_z(g, r, b, 2, tiles)
                    score(g, 1)
                if ahead:
                    turn_sel(g1, b1, 0)
                if old:
                    pe.wait_ge(scores_kept, h + 1)
                    hold(pe, mx_made, h + 1, passed)
                    nc.tensor.transpose(scoresT_ps, scores[0:G * H, :], ident[0:G * H, 0:G * H])
                    for s in range(G):
                        i = nc.tensor.matmul(mx_ps[:, s * 3 * H:(s + 1) * 3 * H], selT[c][:, s, :],
                                             mx3[:, s * 3 * H:(s + 1) * 3 * H], start=True, stop=True)
                    i.then_inc(mx_picked, 1)
                if new:
                    sum_z(g, r, b, 3, tiles)
                if ahead:
                    tiles = load_tiles(g1, r1, b1, 0)
                if new:
                    score(g, 2)
                for p in range(G // 2):
                    if old:
                        weigh(h, c, p)
                    if ahead and p == 0:
                        sum_z(g1, r1, b1, 0, tiles)
                    if new and p == 2:
                        score(g, 3)
                    if ahead and p == 4:
                        sum_z(g1, r1, b1, 1, tiles)
                if new:
                    pe.wait_ge(last_made, g + 1)
                    nc.tensor.transpose(lastT_ps, last[0:G * (H + 1), :], ident[0:G * (H + 1), 0:G * (H + 1)]
                                        ).then_inc(last_turned, 1)
                if ahead:
                    turn_sel(g1, b1, 1)
                    pe.wait_ge(scores_kept, g + 1)
                    score(g1, 0)

            tiles = load_tiles(0, 0, 0, 0)
            turn_sel(0, 0, 0)
            for q in range(2):
                sum_z(0, 0, 0, q, tiles)
            turn_sel(0, 0, 1)
            score(0, 0)
            over_iterations(pe, body)

        @block.scalar
        def _(act):
            def make_idx(g, b):
                nc.scalar.copy(idx[b], m["srcs"][:, bass.ds(g * G, G)]).then_inc(idx_ready, 1)

            def keep_selT(g, b, half):
                act.wait_ge(selT_turned, g * 2 + (half + 1))
                nc.scalar.copy(selT[b][:, half * (G // 2):(half + 1) * (G // 2), :],
                               t_ps[:, :].rearrange("p (s e) -> p s e", e=P)).then_inc(selT_made, 1)

            def scale_z(g, q):
                n = g * NQ + q
                act.wait_ge(z_summed, n + 1)
                wait(act, z_scored, n - 1)
                nc.scalar.activation(z[q % 2], z_ps[q % 2][:, :], ACT.Copy, scale=SLOPE).then_inc(z_scaled, 1)

            def widen_sel(g, b, q):
                wait(act, summed, (g - 1) * (G // 2) + 2 * (q + 1))
                nc.scalar.copy(sel32[:, q * Q:(q + 1) * Q, :], sel[b][:, q * Q:(q + 1) * Q, :]
                               ).then_inc(sel32_made, 1)

            def body(g, r, b, new=True, old=True, ahead=True):
                h, c = g - 1, (b + RING - 1) % RING
                g1, b1 = g + 1, (b + 1) % RING
                if ahead:
                    make_idx(g + 2, (b + 2) % RING)
                if old:
                    widen_sel(h, c, 0)
                    widen_sel(h, c, 1)
                if new:
                    scale_z(g, 2)
                if ahead:
                    keep_selT(g1, b1, 0)
                if old:
                    act.wait_ge(grow_in, h + 1)
                    nc.scalar.activation(grow[:, H:2 * H], grow[:, 0:H], ACT.Exp).then_inc(grown, 1)
                    act.wait_ge(diff_made, h + 1)
                    nc.scalar.activation(xg[c][:, :, D:W], diff.rearrange("p (s h) -> p s h", h=H),
                                         ACT.Exp).then_inc(weights, 1)
                if new:
                    scale_z(g, 3)
                if old:
                    widen_sel(h, c, 2)
                if ahead:
                    scale_z(g1, 0)
                if old:
                    widen_sel(h, c, 3)
                if ahead:
                    scale_z(g1, 1)
                if new:
                    act.wait_ge(last_made, g + 1)
                    nc.scalar.copy(scores[0:G * H, :], score_ps[0:G * H, 0:P]).then_inc(scores_kept, 1)
                if ahead:
                    keep_selT(g1, b1, 1)

            make_idx(0, 0)
            make_idx(1, 1)
            keep_selT(0, 0, 0)
            for q in range(2):
                scale_z(0, q)
            keep_selT(0, 0, 1)
            over_iterations(act, body)

        @block.vector
        def _(dve):
            found3 = found.rearrange("p (h s) -> p h s", s=SLOT)
            upmax3 = upmax.rearrange("p (h s) -> p h s", s=SLOT)
            reset3 = reset[:, 0:H * SLOT].rearrange("p (h s) -> p h s", s=SLOT)
            seen3 = seen.rearrange("p (s h) -> p s h", h=H + 1)
            last4 = last3.rearrange("p (s i h) -> p i h s", i=3, h=H + 1)
            lastT3 = lastT_ps.rearrange("p (h s) -> p h s", s=G)
            lrest3 = lrest.rearrange("p (h s) -> p h s", s=G)
            mx4 = mx3.rearrange("p (s i h) -> p i h s", i=3, h=H)
            rest3 = rest.rearrange("p (h s) -> p h s", s=G)

            def build_sel(g, b, s):
                nc.vector.tensor_scalar(sel[b][:, s, :], m["iota_row"][:, :],
                                        m["dloc"][:, bass.ds(g * G + s, 1)], None, ALU.is_equal).then_inc(sel_built, 1)

            def rectify(g, q):
                dve.wait_ge(z_scaled, g * NQ + (q + 1))
                nc.vector.tensor_tensor(z[q % 2], z_ps[q % 2][:, :], z[q % 2], ALU.max).then_inc(z_rect, 1)

            def body(g, r, b, new=True, old=True, ahead=True):
                h, c = g - 1, (b + RING - 1) % RING
                done = [0]

                def mark(ins):
                    done[0] += 1
                    ins.then_inc(chain, 1)

                def settle():
                    dve.wait_ge(chain, h * CHAIN + done[0])

                built = [0]

                def build(count):
                    for _ in range(count if ahead else 0):
                        build_sel(g + 1, (b + 1) % RING, built[0])
                        built[0] += 1

                def link(ins):
                    mark(ins)
                    build(min(1, G - built[0]))
                    settle()

                if old:
                    dve.wait_ge(last_turned, h + 1)
                    link(nc.vector.tensor_copy(last4[:, 0], lastT3))
                    link(nc.vector.tensor_tensor(lrest3, lastT3, last4[:, 0], ALU.subtract))
                    link(nc.vector.tensor_copy(last4[:, 1], lrest3))
                    nc.vector.tensor_tensor(last4[:, 2], lrest3, last4[:, 1], ALU.subtract).then_inc(last_split, 1)
                    build(1)
                    dve.wait_ge(found_made, h + 1)
                    link(nc.vector.tensor_reduce(
                        seen3, seen_ps.rearrange("p (s i h) -> p s h i", i=3, h=H + 1), axis=AX_X, op=ALU.add))
                    link(nc.vector.tensor_scalar(absent, seen3[:, :, H], BIG, -BIG, ALU.mult, ALU.add))
                    link(nc.vector.tensor_tensor(found3[:, :, 1:SLOT],
                                                 seen3[:, :, 0:H].rearrange("p s h -> p h s"),
                                                 absent.unsqueeze(1).to_broadcast([P, H, G]), ALU.add))
                    dve.wait_ge(reset_made, h + 1)
                    link(nc.vector.tensor_tensor_scan(upto, reset[:, 0:H * SLOT], found, RESET, ALU.add, ALU.max))
                    link(nc.vector.tensor_tensor_scan(upmax[:, ::-1], reset[:, 1:H * SLOT + 1][:, ::-1],
                                                      upto[:, ::-1], RESET, ALU.add, ALU.max))
                    mark(nc.vector.tensor_copy(mx4[:, 0], upmax3[:, :, 1:SLOT]))
                    nc.vector.tensor_tensor(grow[:, 0:H], found3[:, :, 0], upmax3[:, :, 0],
                                            ALU.subtract).then_inc(grow_in, 1)
                    settle()
                    link(nc.vector.tensor_tensor(rest3, upmax3[:, :, 1:SLOT], mx4[:, 0], ALU.subtract))
                    link(nc.vector.tensor_copy(mx4[:, 1], rest3))
                    nc.vector.tensor_tensor(mx4[:, 2], rest3, mx4[:, 1], ALU.subtract).then_inc(mx_made, 1)
                    dve.wait_ge(grow_in, h + 1)
                    mark(nc.vector.tensor_copy(found3[:, :, 0], upmax3[:, :, G]))
                else:
                    build(G)
                if new:
                    rectify(g, 2)
                if old:
                    _, tiles = nc.values_load_multi_w_load_instructions(
                        offs[c][0:1, SLOT:2 * SLOT], engines=(DVE,), min_val=0, max_val=(TILES - 1) * W,
                        skip_runtime_bounds_check_because="the tile is held below TILES")
                    dve.wait_ge(mx_picked, h + 1)
                    link(nc.vector.tensor_reduce(
                        mx.rearrange("p (s h) -> p s h", h=H),
                        mx_ps.rearrange("p (s i h) -> p s h i", i=3, h=H), axis=AX_X, op=ALU.add))
                    link(nc.vector.tensor_tensor(
                        diff.rearrange("p (s h) -> p s h", h=H), scoresT_ps.rearrange("p (h s) -> p s h", s=G),
                        mx.rearrange("p (s h) -> p s h", h=H), ALU.subtract))
                    nc.vector.tensor_scalar(diff, diff, 0.0, None, ALU.min).then_inc(diff_made, 1)
                    dve.wait_ge(grown, h + 1)
                    wait(dve, folded, h * FOLDS)
                    carried = m["sums"][:, bass.ds(tiles[0], W)]
                    msg4 = carried[:, 0:D].rearrange("p (h c) -> p h c", h=H)
                    mark(nc.vector.tensor_tensor(msg4, msg4, grow[:, H:2 * H].unsqueeze(2).to_broadcast([P, H, C]),
                                                 ALU.mult))
                    nc.vector.tensor_tensor(carried[:, D:W], carried[:, D:W], grow[:, H:2 * H],
                                            ALU.mult).then_inc(folded, 1)
                    dve.wait_ge(weights, h + 1)

                def weight_messages(s):
                    x3 = xg[c][:, s, 0:D].rearrange("p (h c) -> p h c", h=H)
                    nc.vector.tensor_tensor(x3, x3, xg[c][:, s, D:W].unsqueeze(2).to_broadcast([P, H, C]),
                                            ALU.mult).then_inc(messages, 1)

                def fold(s):
                    if s % 2 == 0:
                        dve.wait_ge(summed, h * (G // 2) + (s // 2 + 1))
                    dve.wait_ge(folded, h * FOLDS + (s + 1))
                    to = m["sums"][:, bass.ds(tiles[s + 1], W)]
                    nc.vector.tensor_tensor(to, to, o_ps[(c * (G // 2) + s // 2) % 3][:, (s % 2) * W:(s % 2 + 1) * W],
                                            ALU.add).then_inc(folded, 1)

                if old:
                    for s in range(LEAD):
                        weight_messages(s)
                    settle()
                if new:
                    rectify(g, 3)
                for s in range(G):
                    if old:
                        fold(s)
                        if s + LEAD < G:
                            weight_messages(s + LEAD)
                    if ahead and s == 10:
                        rectify(g + 1, 0)
                    if new and s == 11:
                        dve.wait_ge(control[b], r * CONTROL + CONTROL)
                        dve.wait_ge(z_scored, g * NQ + NQ)
                        nc.vector.tensor_tensor_scan(running[0:G * H, :], flags[b][0:G * H, 0:P],
                                                     score_ps[0:G * H, 0:P], RESET, ALU.add, ALU.max
                                                     ).then_inc(scanned, 1)
                    if new and s == 13:
                        dve.wait_ge(scanned, g + 1)
                        nc.vector.tensor_tensor(last[0:G * (H + 1), :], running[0:G * (H + 1), :],
                                                flags[b][0:G * (H + 1), P:2 * P], ALU.mult).then_inc(last_made, 1)
                    if new and s == 12:
                        nc.vector.tensor_copy(reset3[:, :, 1:SLOT],
                                              r0[:, bass.ds(g * G, G)].unsqueeze(1).to_broadcast([P, H, G])
                                              ).then_inc(reset_made, 1)
                    if s in (12, 14):
                        build(min(2, G - built[0]))
                if ahead:
                    build(G - built[0])
                    rectify(g + 1, 1)
                assert not old or done[0] == CHAIN, done[0]

            nc.vector.memset(m["sums"][:, :], 0.0).then_inc(zeroed, 1)
            nc.vector.memset(found, -BIG).then_inc(zeroed, 1)
            nc.vector.memset(running, 1.0).then_inc(zeroed, 1)
            nc.vector.memset(reset, RESET).then_inc(zeroed, 1)
            for s in range(G):
                build_sel(0, 0, s)
            dve.wait_ge(zeroed, 4)
            rectify(0, 0)
            rectify(0, 1)
            over_iterations(dve, body)

    nc.clear_and_free_semaphores(sems)
    nc.all_engine_barrier()


def dense(nc, a, m, layer, xl_table, out):
    final = out is not None
    ctx = ExitStack()
    with ctx:
        def sem(name):
            return ctx.enter_context(nc.semaphore(f"d{layer}_{name}"))

        area = Area(m["work"])
        B = BT * P
        h = area.take(B)
        hT = area.take(B)
        u = area.take(FB * Q * P).rearrange("p (f n) -> p f n", f=FB)
        y = area.take(B)
        yT = area.take(B)
        xres = area.take(B)
        both = area.take(BT * 2 * D)
        w1 = area.take(F)
        w2 = area.take(F).rearrange("p (f d) -> p f d", f=FB)
        b1 = area.take(FB)
        rows = area.take(4 * D).rearrange("p (k d) -> p k d", k=4)
        den = area.take(BT * H)
        stats = area.take(BT * 6)
        norm = area.take(BT * 2)
        dev = area.take(BT)
        eps = area.take(1)
        turn_ps = [ctx.enter_context(nc.psum_tensor(f"d{layer}_t{i}", [P, 512], F32)) for i in range(2)]
        u_ps = [ctx.enter_context(nc.psum_tensor(f"d{layer}_u{i}", [P, 512], F32)) for i in range(FB)]
        y_ps = [ctx.enter_context(nc.psum_tensor(f"d{layer}_y{i}", [P, 512], F32)) for i in range(2)]
        HALVES = ((0, Q), (Q, BT))

        names = ("weights_in", "x_in", "h_made", "h_turned", "hT_kept", "u_made", "u_kept", "y_made", "y_added",
                 "chain", "var_made", "dev_made", "normed", "y_turned", "yT_kept", "projected", "added",
                 "hi", "rest1", "mid", "low", "stored", "att0", "passed", "y_free")
        (weights_in, x_in, h_made, h_turned, hT_kept, u_made, u_kept, y_made, y_added, chain, var_made, dev_made,
         normed, y_turned, yT_kept, projected, added, hi, rest1, mid, low, stored, att0, passed, y_free) = (sem(s) for s in names)
        CHAIN = 3 + 3 + 4 + (3 if final else 0)
        NORMS = 2 if final else 1
        LOADS = 16 * 7
        block = ctx.enter_context(nc.Block())
        x3 = parts_view(m)
        sums3 = m["sums"][:, :].rearrange("p (t w) -> p t w", w=W)
        f_, l_ = f"f{layer}_", f"ln{layer}_"

        def rows_of(dram, k):
            return dram[bass.ds(k * B, B), :].rearrange("(t p) d -> p t d", p=P)

        @block.sync
        def _(sp):
            sp.dma_start(w1, a[f_ + "w1"]).then_inc(weights_in, 16)
            sp.dma_start(w2, a[f_ + "w2"].rearrange("(f p) d -> p f d", p=P)).then_inc(weights_in, 16)
            sp.dma_start(b1, a[f_ + "b1"]).then_inc(weights_in, 16)
            for k, name in enumerate((f"c{layer}_bias", f_ + "b2", l_ + "g", l_ + "b")):
                sp.dma_start(rows[:, k, :], a[name].partition_broadcast(P)).then_inc(weights_in, 16)
            if not final:
                load_projection(sp, a, m, 2, weights_in)
            else:
                with sp.Fori(0, BATCHES) as k:
                    sp.wait_ge(h_made, k + 1)
                    sp.dma_start(xres.rearrange("p (t d) -> p t d", t=BT), rows_of(a["x"], k)).then_inc(x_in, 16)

        @block.gpsimd
        def _(pool):
            with pool.Fori(0, BATCHES) as k:
                if final:
                    pool.wait_ge(normed, k * NORMS + NORMS)
                    pool.dma_start(rows_of(out, k), y.rearrange("p (t d) -> p t d", t=BT)).then_inc(stored, 16)
                else:
                    pool.wait_ge(added, k * BT + BT)
                    pool.dma_start(rows_of(xl_table, k),
                                   both.rearrange("p (t d) -> p t d", t=BT)[:, :, 0:D]).then_inc(stored, 16)
                pool.wait_ge(stored, k * 16 + 16)
                pool.sem_inc(y_free, 1)

        @block.tensor
        def _(pe):
            ident = m["ident"][:, :]
            pe.wait_ge(weights_in, LOADS + (0 if final else 16 * (4 + H)))

            def turn(src, done):
                for n, (lo, hi_) in enumerate(HALVES):
                    for j in range(lo, hi_):
                        i = nc.tensor.transpose(turn_ps[n][:, (j - lo) * P:(j - lo + 1) * P],
                                                src[:, j * P:(j + 1) * P], ident)
                    i.then_inc(done, 1)

            with pe.Fori(0, BATCHES) as k:
                pe.wait_ge(h_made, k + 1)
                turn(h, h_turned)
                for n, (lo, hi_) in enumerate(HALVES):
                    cols = slice(lo * P, hi_ * P)
                    pe.wait_ge(hT_kept, k * 2 + (n + 1))
                    for f in range(FB):
                        if n:
                            pe.wait_ge(u_kept, k * 2 * FB + (f + 1))
                        nc.tensor.matmul(u_ps[f][:, 0:(hi_ - lo) * P], w1[:, f * P:(f + 1) * P], hT[:, cols],
                                         start=True, stop=True).then_inc(u_made, 1)
                    pe.wait_ge(u_kept, k * 2 * FB + (n * FB + FB))
                    for j in range(lo, hi_):
                        at = slice((j - lo) * P, (j - lo + 1) * P)
                        for f in range(FB):
                            i = nc.tensor.matmul(y_ps[n][:, at], u[:, f, at], w2[:, f, :],
                                                 start=(f == 0), stop=(f == FB - 1))
                    i.then_inc(y_made, 1)
                if not final:
                    pe.wait_ge(normed, k + 1)
                    turn(y, y_turned)
                    pe.wait_ge(yT_kept, k * 2 + 2)
                    for j in range(BT):
                        i = nc.tensor.matmul(u_ps[j % FB][:, (j // FB) * 2 * D:(j // FB + 1) * 2 * D],
                                             yT[:, j * P:(j + 1) * P], m["wproj"][:, :], start=True, stop=True)
                    i.then_inc(projected, 1)

        @block.scalar
        def _(act):
            act.wait_ge(weights_in, LOADS + (0 if final else 16 * (4 + H)))
            with act.Fori(0, BATCHES) as k:
                for n, (lo, hi_) in enumerate(HALVES):
                    act.wait_ge(h_turned, k * 2 + (n + 1))
                    nc.scalar.copy(hT[:, lo * P:hi_ * P], turn_ps[n][:, 0:(hi_ - lo) * P]).then_inc(hT_kept, 1)
                for n, (lo, hi_) in enumerate(HALVES):
                    if n:
                        act.wait_ge(y_made, k * 2 + 1)
                    for f in range(FB):
                        act.wait_ge(u_made, k * 2 * FB + (n * FB + f + 1))
                        nc.scalar.activation(u[:, f, 0:(hi_ - lo) * P], u_ps[f][:, 0:(hi_ - lo) * P], ACT.Relu,
                                             bias=b1[:, f:f + 1]).then_inc(u_kept, 1)
                for r in range(NORMS):
                    act.wait_ge(var_made, k * NORMS + (r + 1))
                    nc.scalar.activation(dev, norm[:, 1:2 * BT:2], ACT.Sqrt, bias=eps).then_inc(dev_made, 1)
                if not final:
                    for n, (lo, hi_) in enumerate(HALVES):
                        act.wait_ge(y_turned, k * 2 + (n + 1))
                        nc.scalar.copy(yT[:, lo * P:hi_ * P], turn_ps[n][:, 0:(hi_ - lo) * P]).then_inc(yT_kept, 1)
                    rest = both.rearrange("p (t d) -> p t d", t=BT)[:, :, D:2 * D]
                    tiles = bass.ds(k * BT, BT)
                    act.wait_ge(added, k * BT + BT)
                    nc.scalar.copy(x3[:, tiles, 0, :], rest).then_inc(hi, 1)
                    act.wait_ge(rest1, k + 1)
                    nc.scalar.copy(x3[:, tiles, 1, :], rest).then_inc(mid, 1)

        @block.vector
        def _(dve):
            nc.vector.memset(eps, EPS).then_inc(att0, 1)
            dve.sem_inc(y_free, 1)
            dve.wait_ge(att0, 1)
            dve.wait_ge(weights_in, LOADS + (0 if final else 16 * (4 + H)))
            h3 = h.rearrange("p (t d) -> p t d", t=BT)
            y3 = y.rearrange("p (t d) -> p t d", t=BT)
            norm3 = norm.rearrange("p (t k) -> p t k", k=2)

            def all_tiles(k):
                return rows[:, k, :].unsqueeze(1).to_broadcast([P, BT, D])

            with dve.Fori(0, BATCHES) as k:
                done = [0]

                def link(ins):
                    done[0] += 1
                    ins.then_inc(chain, 1)
                    dve.wait_ge(chain, k * CHAIN + done[0])

                def normalize(r, affine):
                    for j in range(BT):
                        i = nc.vector.bn_stats(stats[:, j * 6:(j + 1) * 6], y3[:, j, :])
                    link(i)
                    dve.sem_inc(passed, 1)
                    for j in range(BT - 1):
                        nc.vector.bn_aggr(norm3[:, j, :], stats[:, j * 6:(j + 1) * 6])
                    nc.vector.bn_aggr(norm3[:, BT - 1, :], stats[:, (BT - 1) * 6:BT * 6]).then_inc(var_made, 1)
                    dve.wait_ge(var_made, k * NORMS + (r + 1))
                    dve.wait_ge(dev_made, k * NORMS + (r + 1))
                    link(nc.vector.reciprocal(dev, dev))
                    for j in range(BT):
                        ins = nc.vector.tensor_scalar(y3[:, j, :], y3[:, j, :], norm3[:, j, 0:1], dev[:, j:j + 1],
                                                      ALU.subtract, ALU.mult)
                    if not affine:
                        ins.then_inc(normed, 1)
                    else:
                        link(ins)
                        link(nc.vector.tensor_tensor(y3, y3, all_tiles(2), ALU.mult))
                        nc.vector.tensor_tensor(y3, y3, all_tiles(3), ALU.add).then_inc(normed, 1)

                sums = sums3[:, bass.ds(k * BT, BT), :]
                den3 = den.rearrange("p (t h) -> p t h", h=H)
                link(nc.vector.tensor_scalar(den3, sums[:, :, D:W], 1e-16, None, ALU.add))
                link(nc.vector.reciprocal(den, den))
                link(nc.vector.tensor_tensor(
                    h.rearrange("p (t h c) -> p t h c", t=BT, h=H),
                    sums[:, :, 0:D].rearrange("p t (h c) -> p t h c", h=H),
                    den3.unsqueeze(3).to_broadcast([P, BT, H, C]), ALU.mult))
                nc.vector.tensor_tensor(h3, h3, all_tiles(0), ALU.add).then_inc(h_made, 1)
                if final:
                    dve.wait_ge(y_free, k + 1)
                for n, (lo, hi_) in enumerate(HALVES):
                    dve.wait_ge(y_made, k * 2 + (n + 1))
                    link(nc.vector.tensor_tensor(y[:, lo * P:hi_ * P], y_ps[n][:, 0:(hi_ - lo) * P],
                                                 h[:, lo * P:hi_ * P], ALU.add))
                link(nc.vector.tensor_tensor(y3, y3, all_tiles(1), ALU.add))
                normalize(0, True)
                if final:
                    dve.wait_ge(normed, k * NORMS + 1)
                    dve.wait_ge(x_in, k * 16 + 16)
                    link(nc.vector.tensor_tensor(y, y, xres, ALU.add))
                    normalize(1, False)
                else:
                    dve.wait_ge(projected, k + 1)
                    b3 = both.rearrange("p (t d) -> p t d", t=BT)
                    for j in range(BT):
                        nc.vector.tensor_tensor(b3[:, j, :], u_ps[j % FB][:, (j // FB) * 2 * D:(j // FB + 1) * 2 * D],
                                                m["bproj"][:, :], ALU.add).then_inc(added, 1)
                    rest = b3[:, :, D:2 * D]
                    tiles = bass.ds(k * BT, BT)
                    dve.wait_ge(hi, k + 1)
                    nc.vector.tensor_tensor(rest, rest, x3[:, tiles, 0, :], ALU.subtract).then_inc(rest1, 1)
                    dve.wait_ge(mid, k + 1)
                    nc.vector.tensor_tensor(x3[:, tiles, 2, :], rest, x3[:, tiles, 1, :], ALU.subtract).then_inc(low, 1)
                    dve.wait_ge(low, k + 1)
                    dve.wait_ge(stored, k * 16 + 16)
                assert done[0] == CHAIN, (done[0], CHAIN)


def kernel(**inputs):
    import numpy as np
    import concourse.bacc as bacc
    from concourse.bass_utils import run_bass_kernel_spmd

    given = {k.removeprefix("L0_gnn_"): np.asarray(v) for k, v in inputs.items()}
    x = np.zeros((NP, D), np.float32)
    x[:N] = given["x"]
    src = np.zeros(((CHUNKS + 1) * P,), np.int32)
    dst = np.full(((CHUNKS + 1) * P,), NP - 1, np.int32)
    src[:E], dst[:E] = given["src"], given["dst"]
    src, dst = src.reshape(-1, P), dst.reshape(-1, P)
    arrays = {"x": x, "xT": np.ascontiguousarray(x.T), "src_chunks": src, "dst_chunks": dst,
              "last_dst": np.ascontiguousarray(dst[:CHUNKS, P - 1])}
    for k, v in given.items():
        if k in ("x", "src", "dst"):
            continue
        if k.endswith("_att"):
            v = v.reshape(H * C, 1)
        elif k.endswith("_b1"):
            v = np.ascontiguousarray(v.reshape(FB, P).T)
        arrays[k] = v

    nc = bacc.Bacc("TRN2", target_bir_lowering=False, num_devices=1)
    a = {k: nc.dram_tensor("in_" + k, v.shape, mybir.dt.from_np(v.dtype), kind="ExternalInput").ap()
         for k, v in arrays.items()}
    out = nc.dram_tensor("out", [NP, D], F32, kind="ExternalOutput").ap()
    build(nc, a, out)
    r = run_bass_kernel_spmd(nc, [{"in_" + k: v for k, v in arrays.items()}], core_ids=[0])
    return r.results[0]["out"][:N]
```

```python
from contextlib import ExitStack

import concourse.bass as bass
from concourse import mybir

F32 = mybir.dt.float32
BF16 = mybir.dt.bfloat16
I32 = mybir.dt.int32
I16 = mybir.dt.int16
ALU = mybir.AluOpType
ACT = mybir.ActivationFunctionType
AX_X = mybir.AxisListType.X
DVE = mybir.EngineType.DVE
PE = mybir.EngineType.PE

P = 128
N = 12500
D = 128
H, C = 4, 32
F = 512
E = 200000
TILES = -(-N // P)
NP = TILES * P
CHUNKS = -(-E // P)
G = 16
SB = 13
STEPS = SB * P
GROUPS = STEPS // G
Q = 4
NQ = G // Q
W = D + H
RING = 3
BIG = 1.0e30
RESET = -1.0e38
EPS = 1e-5
SLOPE = 0.2
SLOT = G + 1
BT = 7
BATCHES = TILES // BT
FB = F // P
assert STEPS >= CHUNKS + TILES - 1 and GROUPS * G == STEPS and BATCHES * BT == TILES


def wait(eng, sem, value):
    if isinstance(value, int) and value <= 0:
        return
    eng.wait_ge(sem, value)


def hold(eng, sem, value, passed):
    wait(eng, sem, value)
    eng.sem_inc(passed, 1)


def build(nc, a, out):
    top = ExitStack()
    with top:
        def sb(name, shape, dt):
            return top.enter_context(nc.sbuf_tensor(name, shape, dt))

        def sem(name):
            return top.enter_context(nc.semaphore(name))

        xl_table = nc.dram_tensor("xl_table", [NP, D], F32).ap()
        flag_rows = nc.dram_tensor("flag_rows", [STEPS, 2 * P], BF16).ap()
        tile_of_step = nc.dram_tensor("tile_of_step", [SB, P], F32).ap()
        tile_offsets = nc.dram_tensor("tile_offsets", [2, STEPS + 1], I32).ap()

        m = {}
        m["xr3"] = sb("xr3", [P, TILES * 3 * D], BF16)
        m["sums"] = sb("sums", [P, TILES * W], F32)
        m["srcs"] = sb("srcs", [P, STEPS + 2 * G], I16)
        m["dloc"] = sb("dloc", [P, STEPS], BF16)
        m["resets"] = sb("resets", [P, STEPS], BF16)
        m["ident"] = sb("ident", [P, P], F32)
        m["ident16"] = sb("ident16", [P, P], BF16)
        m["iota_row"] = sb("iota_row", [P, P], BF16)
        m["wproj"] = sb("wproj", [P, 2 * D], F32)
        m["bproj"] = sb("bproj", [P, 2 * D], F32)
        m["att"] = sb("att", [P, G * H + G - 1], F32)
        WORK = 72384
        m["work"] = sb("work", [P, WORK // 4], F32)

        prepare(nc, a, m, flag_rows, tile_of_step, tile_offsets)
        project_input(nc, a, m, xl_table)
        edges(nc, a, m, 1, xl_table, flag_rows, tile_offsets)
        dense(nc, a, m, 1, xl_table, None)
        edges(nc, a, m, 2, xl_table, flag_rows, tile_offsets)
        dense(nc, a, m, 2, None, out)


class Area:

    def __init__(self, work):
        self.work, self.at = work, 0

    def take(self, columns, dt=F32):
        size = {F32: 4, I32: 4, BF16: 2, I16: 2}[dt]
        words = -(-columns * size // 4)
        v = self.work[:, self.at:self.at + words]
        self.at += words
        assert self.at <= self.work.shape[1], self.at
        return v if dt == F32 else v.bitcast(dt)[:, 0:columns]


def prepare(nc, a, m, flag_rows, tile_of_step, tile_offsets):
    ctx = ExitStack()
    with ctx:
        def sem(name):
            return ctx.enter_context(nc.semaphore("p_" + name))

        area = Area(m["work"])
        last_dst = area.take(CHUNKS, I32)
        end_tile = area.take(CHUNKS, I32)
        chunk_no = area.take(CHUNKS, I32)
        end_step = area.take(CHUNKS)
        chunk_f = area.take(CHUNKS)
        before = area.take(CHUNKS)
        step_i = area.take(SB, I32)
        step_no = area.take(SB)
        chunk_of = area.take(SB)
        tile_of = area.take(SB)
        tile_base = area.take(SB)
        chunk_idx = area.take(SB, I32)
        iota_i = area.take(P, I32)
        tcol = area.take(P)
        prep2 = area.at
        area2 = Area(m["work"])
        area2.at = prep2
        tiles_b = area.take(STEPS)
        trow = area.take(2 * (STEPS + 1), I32)
        src_i = m["sums"][:, 0:STEPS].bitcast(I32)
        dst_i = m["sums"][:, STEPS:2 * STEPS].bitcast(I32)
        src_f = m["sums"][:, 2 * STEPS:3 * STEPS]
        dst_f = m["sums"][:, 3 * STEPS:4 * STEPS]
        dloc_f = m["sums"][:, 4 * STEPS:5 * STEPS]
        flags = m["sums"][:, 5 * STEPS:6 * STEPS + STEPS].bitcast(BF16)[:, 0:2 * STEPS]
        ps = [ctx.enter_context(nc.psum_tensor(f"p_ps{i}", [P, 512], F32)) for i in range(2)]

        loaded, iotas, stair = sem("loaded"), sem("iotas"), sem("stair")
        ident0, gathered, tiles_out, tiles_in = sem("ident0"), sem("gathered"), sem("tiles_out"), sem("tiles_in")
        turned, moved, rows_out, flags_out, v = sem("turned"), sem("moved"), sem("rows_out"), sem("flags_out"), sem("v")
        tables, tT, tC = sem("tables"), sem("tT"), sem("tC")
        block = ctx.enter_context(nc.Block())

        @block.sync
        def _(sp):
            sp.dma_start(last_dst, a["last_dst"].partition_broadcast(P)).then_inc(loaded, 16)
            sp.wait_ge(tC, 1)
            sp.dma_start(tile_of_step, tcol[0:SB, :]).then_inc(tiles_out, 16)
            sp.wait_ge(tiles_out, 16)
            sp.dma_start(tiles_b, tile_of_step.rearrange("k p -> (k p)").partition_broadcast(P)).then_inc(tiles_in, 16)
            sp.wait_ge(rows_out, 1)
            sp.dma_start(tile_offsets.rearrange("a b -> (a b)").partition_broadcast(1), trow[0:1, :]).then_inc(flags_out, 16)
            sp.wait_ge(tables, 1)
            sp.dma_start(flag_rows.rearrange("(k p) f -> p k f", p=P),
                         flags.rearrange("p (k f) -> p k f", k=SB)).then_inc(flags_out, 16)
            sp.wait_ge(flags_out, 32)

        @block.gpsimd
        def _(pool):
            nc.gpsimd.iota(chunk_no, pattern=[[1, CHUNKS]], base=0, channel_multiplier=0).then_inc(iotas, 1)
            nc.gpsimd.iota(step_i, pattern=[[P, SB]], base=0, channel_multiplier=1).then_inc(iotas, 1)
            nc.gpsimd.iota(iota_i, pattern=[[1, P]], base=0, channel_multiplier=0).then_inc(iotas, 1)
            nc.gpsimd.memset(m["ident"][:, :], 0.0).then_inc(ident0, 1)
            pool.wait_ge(ident0, 1)
            nc.gpsimd.affine_select(out=m["ident"][:, :], in_=m["ident"][:, :], compare_op=ALU.not_equal,
                                    fill=1.0, base=0, pattern=[[-1, P]], channel_multiplier=1).then_inc(ident0, 1)
            pool.wait_ge(stair, 1)
            for k in range(SB):
                for rows, name in ((src_i, "src_chunks"), (dst_i, "dst_chunks")):
                    nc.gpsimd.indirect_dma_start(
                        out=rows[:, k * P:(k + 1) * P], out_offset=None, in_=a[name],
                        in_offset=bass.IndirectOffsetOnAxis(ap=chunk_idx[:, k:k + 1], axis=0)).then_inc(gathered, 16)
            pool.wait_ge(gathered, 32 * SB)

        @block.vector
        def _(dve):
            n = [0]

            def link(ins):
                n[0] += 1
                ins.then_inc(v, 1)
                dve.wait_ge(v, n[0])

            dve.wait_ge(ident0, 2)
            link(nc.vector.tensor_copy(m["ident16"][:, :], m["ident"][:, :]))
            dve.wait_ge(iotas, 3)
            link(nc.vector.tensor_copy(m["iota_row"][:, :], iota_i))
            link(nc.vector.memset(m["srcs"][:, STEPS:], 0))
            link(nc.vector.tensor_copy(step_no, step_i))
            link(nc.vector.tensor_copy(chunk_f, chunk_no))
            dve.wait_ge(loaded, 16)
            link(nc.vector.tensor_scalar(end_tile, last_dst, 7, None, ALU.arith_shift_right))
            link(nc.vector.tensor_copy(end_step, end_tile))
            link(nc.vector.tensor_tensor(end_step, end_step, chunk_f, ALU.add))
            for k in range(SB):
                link(nc.vector.tensor_scalar(before, end_step, step_no[:, k:k + 1], None, ALU.is_lt))
                link(nc.vector.tensor_reduce(chunk_of[:, k:k + 1], before, axis=AX_X, op=ALU.add))
            link(nc.vector.tensor_tensor(tile_of, step_no, chunk_of, ALU.subtract))
            link(nc.vector.tensor_scalar(tile_of, tile_of, float(TILES - 1), None, ALU.min))
            link(nc.vector.tensor_scalar(tile_base, tile_of, float(P), None, ALU.mult))
            nc.vector.tensor_copy(chunk_idx, chunk_of).then_inc(stair, 1)
            dve.wait_ge(tT, 1)
            nc.vector.tensor_copy(tcol[0:SB, :], ps[0][0:SB, 0:P]).then_inc(tC, 1)
            dve.wait_ge(tiles_in, 16)
            link(nc.vector.memset(m["resets"][:, 0:1], 0.0))
            link(nc.vector.tensor_tensor(m["resets"][:, 1:STEPS], tiles_b[:, 1:STEPS], tiles_b[:, 0:STEPS - 1],
                                         ALU.not_equal))
            link(nc.vector.tensor_scalar(m["resets"][:, :], m["resets"][:, :], RESET, None, ALU.mult))
            link(nc.vector.memset(trow[0:1, :], 0))
            link(nc.vector.tensor_scalar(trow[0:1, 1:STEPS + 1], tiles_b[0:1, :], float(3 * D), None, ALU.mult))
            nc.vector.tensor_scalar(trow[0:1, STEPS + 2:2 * STEPS + 2], tiles_b[0:1, :], float(W), None,
                                    ALU.mult).then_inc(rows_out, 1)
            dve.wait_ge(gathered, 32 * SB)
            link(nc.vector.tensor_copy(src_f, src_i))
            link(nc.vector.tensor_copy(dst_f, dst_i))
            for k in range(SB):
                c = slice(k * P, (k + 1) * P)
                link(nc.vector.tensor_scalar(dloc_f[:, c], dst_f[:, c], tile_base[:, k:k + 1], None, ALU.subtract))
            d3 = dst_f.rearrange("p (k e) -> p k e", k=SB)
            f4 = flags.rearrange("p (k w e) -> p k w e", k=SB, w=2)
            link(nc.vector.tensor_tensor(f4[:, :, 0, 1:P], d3[:, :, 1:P], d3[:, :, 0:P - 1], ALU.not_equal))
            link(nc.vector.tensor_copy(f4[:, :, 1, 0:P - 1], f4[:, :, 0, 1:P]))
            link(nc.vector.memset(f4[:, :, 0, 0:1], 1.0))
            link(nc.vector.memset(f4[:, :, 1, P - 1:P], 1.0))
            nc.vector.tensor_scalar(f4[:, :, 0, :], f4[:, :, 0, :], RESET, None, ALU.mult).then_inc(tables, 1)
            nc.vector.tensor_copy(dloc_f[:, 0:1], dloc_f[:, 0:1]).then_inc(turned, 1)
            for k in range(SB):
                dve.wait_ge(moved, k + 1)
                c = slice(k * P, (k + 1) * P)
                link(nc.vector.tensor_copy(m["srcs"][:, c], ps[k % 2][:, 0:P]))
                nc.vector.tensor_copy(m["dloc"][:, c], ps[k % 2][:, P:2 * P]).then_inc(turned, 1)

        @block.tensor
        def _(pe):
            pe.wait_ge(ident0, 2)
            pe.wait_ge(stair, 1)
            nc.tensor.transpose(ps[0][0:SB, 0:P], tile_of, m["ident"][:, :]).then_inc(tT, 1)
            pe.wait_ge(tC, 1)
            for k in range(SB):
                pe.wait_ge(turned, max(1, k))
                c = slice(k * P, (k + 1) * P)
                nc.tensor.transpose(ps[k % 2][:, 0:P], src_f[:, c], m["ident"][:, :])
                nc.tensor.transpose(ps[k % 2][:, P:2 * P], dloc_f[:, c], m["ident"][:, :]).then_inc(moved, 1)


def load_projection(sp, a, m, layer, sem):
    c = f"c{layer}_"
    sp.dma_start(m["wproj"][:, 0:D], a[c + "wl"]).then_inc(sem, 16)
    sp.dma_start(m["wproj"][:, D:2 * D], a[c + "wr"]).then_inc(sem, 16)
    sp.dma_start(m["bproj"][:, 0:D], a[c + "bl"].partition_broadcast(P)).then_inc(sem, 16)
    sp.dma_start(m["bproj"][:, D:2 * D], a[c + "br"].partition_broadcast(P)).then_inc(sem, 16)
    for h in range(H):
        sp.dma_start(m["att"][h * C:(h + 1) * C, (h + 1) * G - 1:(h + 1) * G],
                     a[c + "att"][h * C:(h + 1) * C, :]).then_inc(sem, 16)
    return 16 * (4 + H)


def parts_view(m):
    return m["xr3"][:, :].rearrange("p (t i d) -> p t i d", i=3, d=D)


def project_input(nc, a, m, xl_table):
    ctx = ExitStack()
    with ctx:
        def sem(name):
            return ctx.enter_context(nc.semaphore("i_" + name))

        PAIRS = -(-BT // 2)
        area = Area(m["work"])
        xT = [area.take(BT * P) for _ in range(2)]
        both = [area.take(BT * 2 * D) for _ in range(2)]
        ps = [ctx.enter_context(nc.psum_tensor(f"i_ps{i}", [P, 512], F32)) for i in range(PAIRS)]
        w_in, x_in, att0 = sem("w_in"), [sem("x_in0"), sem("x_in1")], sem("att0")
        made, added, hi, mid, rest1, low, stored, both_free = (
            sem(s) for s in ("made", "added", "hi", "mid", "rest1", "low", "stored", "both_free"))
        block = ctx.enter_context(nc.Block())
        x3 = parts_view(m)

        @block.sync
        def _(sp):
            sp.wait_ge(att0, 1)
            load_projection(sp, a, m, 1, w_in)
            with sp.Fori(0, BATCHES // 2) as it:
                for b in range(2):
                    k = it * 2 + b
                    sp.wait_ge(made, k * PAIRS + PAIRS)
                    sp.dma_start(xT[b], a["xT"][:, bass.ds(k * (BT * P), BT * P)]).then_inc(x_in[b], 16)

        @block.gpsimd
        def _(pool):
            nc.gpsimd.memset(m["att"][:, :], 0.0).then_inc(att0, 1)
            with pool.Fori(0, BATCHES // 2) as it:
                for b in range(2):
                    k = it * 2 + b
                    pool.wait_ge(added, k * PAIRS + 2 * PAIRS)
                    pool.dma_start(xl_table[bass.ds(k * (BT * P), BT * P), :].rearrange("(t p) d -> p t d", p=P),
                                   both[b].rearrange("p (t d) -> p t d", t=BT)[:, :, 0:D]).then_inc(stored, 16)
                    pool.wait_ge(stored, k * 16 + 16)
                    pool.sem_inc(both_free, 1)

        @block.tensor
        def _(pe):
            pe.sem_inc(made, 2 * PAIRS)
            pe.wait_ge(w_in, 16 * (4 + H))
            with pe.Fori(0, BATCHES // 2) as it:
                for b in range(2):
                    k = it * 2 + b
                    pe.wait_ge(x_in[b], it * 16 + 16)
                    for p in range(PAIRS):
                        pe.wait_ge(added, k * PAIRS + (p + 1))
                        for j in range(2 * p, min(2 * p + 2, BT)):
                            i = nc.tensor.matmul(ps[p][:, (j % 2) * 2 * D:(j % 2 + 1) * 2 * D],
                                                 xT[b][:, j * P:(j + 1) * P], m["wproj"][:, :], start=True, stop=True)
                        i.then_inc(made, 1)

        @block.vector
        def _(dve):
            dve.sem_inc(added, PAIRS)
            dve.sem_inc(both_free, 2)
            dve.sem_inc(low, 2)

            def project_pair(it):
                for b in range(2):
                    k = b if it is None else it * 2 + b
                    b3 = both[b].rearrange("p (t d) -> p t d", t=BT)
                    for p in range(PAIRS):
                        t = min(2, BT - 2 * p)
                        dve.wait_ge(made, k * PAIRS + (p + 1 + 2 * PAIRS))
                        if p == 0:
                            dve.wait_ge(both_free, k + 1)
                            if it is not None or b:
                                dve.wait_ge(low, k + 1)
                        nc.vector.tensor_tensor(
                            b3[:, 2 * p:2 * p + t, :], ps[p][:, 0:t * 2 * D].rearrange("p (t d) -> p t d", t=t),
                            m["bproj"][:, :].unsqueeze(1).to_broadcast([P, t, 2 * D]), ALU.add).then_inc(added, 1)
                    if b or it is not None:
                        make_low(k - 1, 1 - b)
                    rest = b3[:, :, D:2 * D]
                    dve.wait_ge(hi, k + 1)
                    nc.vector.tensor_tensor(rest, rest, x3[:, bass.ds(k * BT, BT), 0, :],
                                            ALU.subtract).then_inc(rest1, 1)

            def make_low(j, b):
                rest = both[b].rearrange("p (t d) -> p t d", t=BT)[:, :, D:2 * D]
                tiles = bass.ds(j * BT, BT)
                dve.wait_ge(mid, j + 1)
                nc.vector.tensor_tensor(x3[:, tiles, 2, :], rest, x3[:, tiles, 1, :], ALU.subtract).then_inc(low, 1)

            project_pair(None)
            with dve.Fori(1, BATCHES // 2) as it:
                project_pair(it)
            make_low(BATCHES - 1, 1)

        @block.scalar
        def _(act):
            with act.Fori(0, BATCHES // 2) as it:
                for b in range(2):
                    k = it * 2 + b
                    rest = both[b].rearrange("p (t d) -> p t d", t=BT)[:, :, D:2 * D]
                    tiles = bass.ds(k * BT, BT)
                    act.wait_ge(added, k * PAIRS + 2 * PAIRS)
                    nc.scalar.copy(x3[:, tiles, 0, :], rest).then_inc(hi, 1)
                    act.wait_ge(rest1, k + 1)
                    nc.scalar.copy(x3[:, tiles, 1, :], rest).then_inc(mid, 1)


def edges(nc, a, m, layer, xl_table, flag_rows, tile_offsets):
    ctx = ExitStack()
    with ctx:
        sems = []

        def sem(name):
            sems.append(nc.alloc_semaphore(f"e{layer}_{name}"))
            return sems[-1]

        def pb(name):
            return ctx.enter_context(nc.psum_tensor(f"e{layer}_{name}", [P, 512], F32))

        area = Area(m["work"])
        xg = [area.take(G * W).rearrange("p (s w) -> p s w", s=G) for _ in range(RING)]
        sel = [area.take(G * P, BF16).rearrange("p (s n) -> p s n", s=G) for _ in range(RING)]
        selT = [area.take(G * P, BF16).rearrange("p (s e) -> p s e", s=G) for _ in range(RING)]
        sel32 = area.take(G * P).rearrange("p (s n) -> p s n", s=G)
        flags = [area.take(2 * P, BF16) for _ in range(RING)]
        idx = [area.take(G, I32) for _ in range(RING)]
        offs = [area.take(2 * SLOT, I32) for _ in range(RING)]
        z = [area.take(Q * P) for _ in range(2)]
        scores = area.take(P)
        running = area.take(P)
        last = area.take(P)
        last3 = area.take(G * 3 * (H + 1), BF16)
        lrest = area.take(G * (H + 1))
        seen = area.take(G * (H + 1))
        absent = area.take(G)
        found = area.take(H * SLOT)
        upto = area.take(H * SLOT)
        upmax = area.take(H * SLOT)
        reset = area.take(H * SLOT + 1)
        rest = area.take(H * G)
        mx3 = area.take(G * 3 * H, BF16)
        mx = area.take(G * H)
        diff = area.take(G * H)
        grow = area.take(2 * H)
        z_ps = [pb("z0"), pb("z1")]
        t_ps = ctx.enter_context(nc.psum_tensor(f"e{layer}_t", [P, 1024], BF16))
        score_ps, small_ps = pb("scores"), pb("small")
        o_ps = [pb("o0"), pb("o1"), pb("o2")]
        scoresT_ps = small_ps[:, 0:G * H]
        lastT_ps = small_ps[:, G * H:G * (2 * H + 1)]
        seen_ps = small_ps[:, G * (2 * H + 1):G * (2 * H + 1 + 3 * (H + 1))]
        mx_ps = small_ps[:, G * H:G * 4 * H]

        gathered = [[sem(f"gathered{b}_{q}") for q in range(NQ)] for b in range(RING)]
        control = [sem(f"control{b}") for b in range(RING)]
        idx_ready = sem("idx_ready")
        sel_built, selT_turned, selT_made = sem("sel_built"), sem("selT_turned"), sem("selT_made")
        z_summed, z_scaled, z_rect, z_scored = sem("z_summed"), sem("z_scaled"), sem("z_rect"), sem("z_scored")
        scores_kept, last_made, last_turned = sem("scores_kept"), sem("last_made"), sem("last_turned")
        last_split, sel32_made = sem("last_split"), sem("sel32_made")
        found_made, mx_made, mx_picked, chain = sem("found_made"), sem("mx_made"), sem("mx_picked"), sem("chain")
        grow_in, grown, diff_made, weights = sem("grow_in"), sem("grown"), sem("diff_made"), sem("weights")
        messages, summed, folded, zeroed = sem("messages"), sem("summed"), sem("folded"), sem("zeroed")
        passed, scanned, reset_made = sem("passed"), sem("scanned"), sem("reset_made")
        LEAD = 6
        CHAIN = 15
        FOLDS = G + 1
        block = ctx.enter_context(nc.Block())
        r0 = m["resets"]

        def over_groups(eng, body, head, tail):
            for g in range(head):
                body(g, g // RING, g % RING)
            loops = (tail - head) // RING
            with eng.Fori(0, loops) as it:
                for u in range(RING):
                    body(it * RING + (head + u), it + (head + u) // RING, (head + u) % RING)
            for g in range(head + loops * RING, tail):
                body(g, g // RING, g % RING)

        def over_iterations(eng, body):
            loops = (GROUPS - 3) // RING
            body(0, 0, 0, old=False)
            body(1, 0, 1)
            with eng.Fori(0, loops) as it:
                for u in range(RING):
                    body(it * RING + (2 + u), it + (2 + u) // RING, (2 + u) % RING)
            for g in range(2 + loops * RING, GROUPS):
                body(g, g // RING, g % RING, ahead=(g < GROUPS - 1))
            body(GROUPS, GROUPS // RING, GROUPS % RING, new=False, ahead=False)

        @block.sync
        def _(sp):
            def load(g, r, b):
                wait(sp, folded, g * FOLDS + (1 - 3) * FOLDS)
                for k in range(H + 1):
                    sp.dma_start(flags[b][k * G:(k + 1) * G, :],
                                 flag_rows[bass.ds(g * G, G), :]).then_inc(control[b], 16)
                sp.dma_start(offs[b][0:1, :].rearrange("p (w s) -> p w s", w=2),
                             tile_offsets[:, bass.ds(g * G, SLOT)].rearrange("(p w) s -> p w s", p=1)
                             ).then_inc(control[b], 16)

            over_groups(sp, load, 3, GROUPS)
        CONTROL = 16 * (H + 2)

        @block.gpsimd
        def _(pool):
            def gather(g, r, b):
                hold(pool, idx_ready, g + 1, passed)
                for s in range(G):
                    if s % Q == 0:
                        if not isinstance(g, int) or g >= RING:
                            hold(pool, summed, (g - RING) * (G // 2) + (s + Q) // 2, passed)
                    nc.gpsimd.indirect_dma_start(
                        out=xg[b][:, s, 0:D], out_offset=None, in_=xl_table,
                        in_offset=bass.IndirectOffsetOnAxis(ap=idx[b][:, s:s + 1], axis=0)
                    ).then_inc(gathered[b][s // Q], 16)

            over_groups(pool, gather, 3, GROUPS)

        @block.tensor
        def _(pe):
            ident = m["ident"]
            ident16 = m["ident16"]

            def turn_sel(g, b, half):
                n = g * 2 + half
                pe.wait_ge(sel_built, g * G + (half + 1) * (G // 2))
                wait(pe, selT_made, n)
                for k in range(G // 2):
                    i = nc.tensor.transpose(t_ps[:, k * P:(k + 1) * P], sel[b][:, half * (G // 2) + k, :],
                                            ident16[:, :])
                i.then_inc(selT_turned, 1)

            def sum_z(g, r, b, q, tiles):
                n = g * NQ + q
                hold(pe, gathered[b][q], r * (16 * Q) + 16 * Q, passed)
                pe.wait_ge(selT_made, g * 2 + (q // 2 + 1))
                wait(pe, z_rect, n - 1)
                for k in range(Q):
                    s = q * Q + k
                    zs = z_ps[q % 2][:, k * P:(k + 1) * P]
                    nc.tensor.matmul(zs, xg[b][:, s, 0:D], ident[:, :], is_transpose=True, start=True, stop=False)
                    for i in range(3):
                        last_i = nc.tensor.matmul(zs, m["xr3"][:, bass.ds(tiles[s % (G // 2)] + i * D, D)], selT[b][:, s, :],
                                                  start=False, stop=(i == 2))
                last_i.then_inc(z_summed, 1)

            def score(g, q):
                n = g * NQ + q
                pe.wait_ge(z_rect, n + 1)
                for k in range(Q):
                    s = q * Q + k
                    i = nc.tensor.matmul(score_ps[0:G * H, 0:P],
                                         m["att"][:, G - 1 - s:G - 1 - s + G * H], z[q % 2][:, k * P:(k + 1) * P],
                                         start=(s == 0), stop=(s == G - 1))
                i.then_inc(z_scored, 1)

            def weigh(g, b, p):
                pe.wait_ge(messages, g * G + (2 * p + 2))
                if p % 2 == 0:
                    pe.wait_ge(sel32_made, g * NQ + (p // 2 + 1))
                wait(pe, folded, g * FOLDS + (2 * p - 3) if p >= 3 else (g - 1) * FOLDS + (G - 3 + 2 * p))
                for s in (2 * p, 2 * p + 1):
                    i = nc.tensor.matmul(o_ps[(b * (G // 2) + p) % 3][:, (s % 2) * W:(s % 2 + 1) * W], sel32[:, s, :],
                                         xg[b][:, s, :], start=True, stop=True)
                i.then_inc(summed, 1)

            def load_tiles(g, r, b, half):
                hold(pe, control[b], r * CONTROL + CONTROL, passed)
                _, tiles = nc.values_load_multi_w_load_instructions(
                    offs[b][0:1, 1 + half * (G // 2):1 + (half + 1) * (G // 2)], engines=(PE,), min_val=0,
                    max_val=(TILES - 1) * 3 * D,
                    skip_runtime_bounds_check_because="the tile is held below TILES")
                return tiles

            def body(g, r, b, new=True, old=True, ahead=True):
                h, c = g - 1, (b + RING - 1) % RING
                g1, r1, b1 = g + 1, r + (b + 1) // RING, (b + 1) % RING
                if new:
                    tiles = load_tiles(g, r, b, 1)
                if old:
                    pe.wait_ge(last_split, h + 1)
                    for s in range(G):
                        cols = slice(s * 3 * (H + 1), (s + 1) * 3 * (H + 1))
                        i = nc.tensor.matmul(seen_ps[:, cols], sel[c][:, s, :], last3[:, cols],
                                             start=True, stop=True)
                    i.then_inc(found_made, 1)
                if new:
                    sum_z(g, r, b, 2, tiles)
                    score(g, 1)
                if ahead:
                    turn_sel(g1, b1, 0)
                if old:
                    pe.wait_ge(scores_kept, h + 1)
                    hold(pe, mx_made, h + 1, passed)
                    nc.tensor.transpose(scoresT_ps, scores[0:G * H, :], ident[0:G * H, 0:G * H])
                    for s in range(G):
                        i = nc.tensor.matmul(mx_ps[:, s * 3 * H:(s + 1) * 3 * H], selT[c][:, s, :],
                                             mx3[:, s * 3 * H:(s + 1) * 3 * H], start=True, stop=True)
                    i.then_inc(mx_picked, 1)
                if new:
                    sum_z(g, r, b, 3, tiles)
                if ahead:
                    tiles = load_tiles(g1, r1, b1, 0)
                for p in range(G // 2):
                    if old:
                        weigh(h, c, p)
                    if new and p == 1:
                        score(g, 2)
                    if ahead and p == 4:
                        sum_z(g1, r1, b1, 0, tiles)
                    if new and p == 5:
                        score(g, 3)
                if ahead:
                    sum_z(g1, r1, b1, 1, tiles)
                if new:
                    pe.wait_ge(last_made, g + 1)
                    nc.tensor.transpose(lastT_ps, last[0:G * (H + 1), :], ident[0:G * (H + 1), 0:G * (H + 1)]
                                        ).then_inc(last_turned, 1)
                if ahead:
                    turn_sel(g1, b1, 1)
                    pe.wait_ge(scores_kept, g + 1)
                    score(g1, 0)

            tiles = load_tiles(0, 0, 0, 0)
            turn_sel(0, 0, 0)
            for q in range(2):
                sum_z(0, 0, 0, q, tiles)
            turn_sel(0, 0, 1)
            score(0, 0)
            over_iterations(pe, body)

        @block.scalar
        def _(act):
            def make_idx(g, b):
                nc.scalar.copy(idx[b], m["srcs"][:, bass.ds(g * G, G)]).then_inc(idx_ready, 1)

            def keep_selT(g, b, half):
                act.wait_ge(selT_turned, g * 2 + (half + 1))
                nc.scalar.copy(selT[b][:, half * (G // 2):(half + 1) * (G // 2), :],
                               t_ps[:, :].rearrange("p (s e) -> p s e", e=P)).then_inc(selT_made, 1)

            def scale_z(g, q):
                n = g * NQ + q
                act.wait_ge(z_summed, n + 1)
                wait(act, z_scored, n - 1)
                nc.scalar.activation(z[q % 2], z_ps[q % 2][:, :], ACT.Copy, scale=SLOPE).then_inc(z_scaled, 1)

            def widen_sel(g, b, q):
                wait(act, summed, (g - 1) * (G // 2) + 2 * (q + 1))
                nc.scalar.copy(sel32[:, q * Q:(q + 1) * Q, :], sel[b][:, q * Q:(q + 1) * Q, :]
                               ).then_inc(sel32_made, 1)

            def body(g, r, b, new=True, old=True, ahead=True):
                h, c = g - 1, (b + RING - 1) % RING
                g1, b1 = g + 1, (b + 1) % RING
                if ahead:
                    make_idx(g + 2, (b + 2) % RING)
                if old:
                    widen_sel(h, c, 0)
                    widen_sel(h, c, 1)
                if new:
                    scale_z(g, 2)
                if ahead:
                    keep_selT(g1, b1, 0)
                if old:
                    act.wait_ge(grow_in, h + 1)
                    nc.scalar.activation(grow[:, H:2 * H], grow[:, 0:H], ACT.Exp).then_inc(grown, 1)
                    act.wait_ge(diff_made, h + 1)
                    nc.scalar.activation(xg[c][:, :, D:W], diff.rearrange("p (s h) -> p s h", h=H),
                                         ACT.Exp).then_inc(weights, 1)
                if new:
                    scale_z(g, 3)
                if old:
                    widen_sel(h, c, 2)
                    widen_sel(h, c, 3)
                if ahead:
                    scale_z(g1, 0)
                if new:
                    act.wait_ge(last_made, g + 1)
                    nc.scalar.copy(scores[0:G * H, :], score_ps[0:G * H, 0:P]).then_inc(scores_kept, 1)
                if ahead:
                    scale_z(g1, 1)
                    keep_selT(g1, b1, 1)

            make_idx(0, 0)
            make_idx(1, 1)
            keep_selT(0, 0, 0)
            for q in range(2):
                scale_z(0, q)
            keep_selT(0, 0, 1)
            over_iterations(act, body)

        @block.vector
        def _(dve):
            found3 = found.rearrange("p (h s) -> p h s", s=SLOT)
            upmax3 = upmax.rearrange("p (h s) -> p h s", s=SLOT)
            reset3 = reset[:, 0:H * SLOT].rearrange("p (h s) -> p h s", s=SLOT)
            seen3 = seen.rearrange("p (s h) -> p s h", h=H + 1)
            last4 = last3.rearrange("p (s i h) -> p i h s", i=3, h=H + 1)
            lastT3 = lastT_ps.rearrange("p (h s) -> p h s", s=G)
            lrest3 = lrest.rearrange("p (h s) -> p h s", s=G)
            mx4 = mx3.rearrange("p (s i h) -> p i h s", i=3, h=H)
            rest3 = rest.rearrange("p (h s) -> p h s", s=G)

            def build_sel(g, b, s):
                nc.vector.tensor_scalar(sel[b][:, s, :], m["iota_row"][:, :],
                                        m["dloc"][:, bass.ds(g * G + s, 1)], None, ALU.is_equal).then_inc(sel_built, 1)

            def rectify(g, q):
                dve.wait_ge(z_scaled, g * NQ + (q + 1))
                nc.vector.tensor_tensor(z[q % 2], z_ps[q % 2][:, :], z[q % 2], ALU.max).then_inc(z_rect, 1)

            def body(g, r, b, new=True, old=True, ahead=True):
                h, c = g - 1, (b + RING - 1) % RING
                done = [0]

                def mark(ins):
                    done[0] += 1
                    ins.then_inc(chain, 1)

                def settle():
                    dve.wait_ge(chain, h * CHAIN + done[0])

                built = [0]

                def build(count):
                    for _ in range(count if ahead else 0):
                        build_sel(g + 1, (b + 1) % RING, built[0])
                        built[0] += 1

                def link(ins):
                    mark(ins)
                    build(min(1, G - built[0]))
                    settle()

                if old:
                    dve.wait_ge(last_turned, h + 1)
                    link(nc.vector.tensor_copy(last4[:, 0], lastT3))
                    link(nc.vector.tensor_tensor(lrest3, lastT3, last4[:, 0], ALU.subtract))
                    link(nc.vector.tensor_copy(last4[:, 1], lrest3))
                    nc.vector.tensor_tensor(last4[:, 2], lrest3, last4[:, 1], ALU.subtract).then_inc(last_split, 1)
                else:
                    build(G)
                if new:
                    rectify(g, 1)
                if old:
                    dve.wait_ge(found_made, h + 1)
                    link(nc.vector.tensor_reduce(
                        seen3, seen_ps.rearrange("p (s i h) -> p s h i", i=3, h=H + 1), axis=AX_X, op=ALU.add))
                    link(nc.vector.tensor_scalar(absent, seen3[:, :, H], BIG, -BIG, ALU.mult, ALU.add))
                    link(nc.vector.tensor_tensor(found3[:, :, 1:SLOT],
                                                 seen3[:, :, 0:H].rearrange("p s h -> p h s"),
                                                 absent.unsqueeze(1).to_broadcast([P, H, G]), ALU.add))
                    dve.wait_ge(reset_made, h + 1)
                    link(nc.vector.tensor_tensor_scan(upto, reset[:, 0:H * SLOT], found, RESET, ALU.add, ALU.max))
                    link(nc.vector.tensor_tensor_scan(upmax[:, ::-1], reset[:, 1:H * SLOT + 1][:, ::-1],
                                                      upto[:, ::-1], RESET, ALU.add, ALU.max))
                    mark(nc.vector.tensor_copy(mx4[:, 0], upmax3[:, :, 1:SLOT]))
                    nc.vector.tensor_tensor(grow[:, 0:H], found3[:, :, 0], upmax3[:, :, 0],
                                            ALU.subtract).then_inc(grow_in, 1)
                    settle()
                    link(nc.vector.tensor_tensor(rest3, upmax3[:, :, 1:SLOT], mx4[:, 0], ALU.subtract))
                    link(nc.vector.tensor_copy(mx4[:, 1], rest3))
                    nc.vector.tensor_tensor(mx4[:, 2], rest3, mx4[:, 1], ALU.subtract).then_inc(mx_made, 1)
                    dve.wait_ge(grow_in, h + 1)
                    mark(nc.vector.tensor_copy(found3[:, :, 0], upmax3[:, :, G]))
                if new:
                    rectify(g, 2)
                if old:
                    _, tiles = nc.values_load_multi_w_load_instructions(
                        offs[c][0:1, SLOT:2 * SLOT], engines=(DVE,), min_val=0, max_val=(TILES - 1) * W,
                        skip_runtime_bounds_check_because="the tile is held below TILES")
                    dve.wait_ge(mx_picked, h + 1)
                    link(nc.vector.tensor_reduce(
                        mx.rearrange("p (s h) -> p s h", h=H),
                        mx_ps.rearrange("p (s i h) -> p s h i", i=3, h=H), axis=AX_X, op=ALU.add))
                    link(nc.vector.tensor_tensor(
                        diff.rearrange("p (s h) -> p s h", h=H), scoresT_ps.rearrange("p (h s) -> p s h", s=G),
                        mx.rearrange("p (s h) -> p s h", h=H), ALU.subtract))
                    nc.vector.tensor_scalar(diff, diff, 0.0, None, ALU.min).then_inc(diff_made, 1)
                    dve.wait_ge(grown, h + 1)
                    wait(dve, folded, h * FOLDS)
                    carried = m["sums"][:, bass.ds(tiles[0], W)]
                    msg4 = carried[:, 0:D].rearrange("p (h c) -> p h c", h=H)
                    mark(nc.vector.tensor_tensor(msg4, msg4, grow[:, H:2 * H].unsqueeze(2).to_broadcast([P, H, C]),
                                                 ALU.mult))
                    nc.vector.tensor_tensor(carried[:, D:W], carried[:, D:W], grow[:, H:2 * H],
                                            ALU.mult).then_inc(folded, 1)
                    dve.wait_ge(weights, h + 1)

                def weight_messages(s):
                    x3 = xg[c][:, s, 0:D].rearrange("p (h c) -> p h c", h=H)
                    nc.vector.tensor_tensor(x3, x3, xg[c][:, s, D:W].unsqueeze(2).to_broadcast([P, H, C]),
                                            ALU.mult).then_inc(messages, 1)

                def fold(s):
                    if s % 2 == 0:
                        dve.wait_ge(summed, h * (G // 2) + (s // 2 + 1))
                    dve.wait_ge(folded, h * FOLDS + (s + 1))
                    to = m["sums"][:, bass.ds(tiles[s + 1], W)]
                    nc.vector.tensor_tensor(to, to, o_ps[(c * (G // 2) + s // 2) % 3][:, (s % 2) * W:(s % 2 + 1) * W],
                                            ALU.add).then_inc(folded, 1)

                if old:
                    for s in range(LEAD):
                        weight_messages(s)
                    settle()
                if new:
                    rectify(g, 3)
                for s in range(G):
                    if old:
                        fold(s)
                        if s + LEAD < G:
                            weight_messages(s + LEAD)
                    if ahead and s == 10:
                        rectify(g + 1, 0)
                    if new and s == 11:
                        dve.wait_ge(control[b], r * CONTROL + CONTROL)
                        dve.wait_ge(z_scored, g * NQ + NQ)
                        nc.vector.tensor_tensor_scan(running[0:G * H, :], flags[b][0:G * H, 0:P],
                                                     score_ps[0:G * H, 0:P], RESET, ALU.add, ALU.max
                                                     ).then_inc(scanned, 1)
                    if new and s == 13:
                        dve.wait_ge(scanned, g + 1)
                        nc.vector.tensor_tensor(last[0:G * (H + 1), :], running[0:G * (H + 1), :],
                                                flags[b][0:G * (H + 1), P:2 * P], ALU.mult).then_inc(last_made, 1)
                    if new and s == 12:
                        nc.vector.tensor_copy(reset3[:, :, 1:SLOT],
                                              r0[:, bass.ds(g * G, G)].unsqueeze(1).to_broadcast([P, H, G])
                                              ).then_inc(reset_made, 1)
                    if s in (12, 14):
                        build(min(2, G - built[0]))
                if ahead:
                    build(G - built[0])
                assert not old or done[0] == CHAIN, done[0]

            nc.vector.memset(m["sums"][:, :], 0.0).then_inc(zeroed, 1)
            nc.vector.memset(found, -BIG).then_inc(zeroed, 1)
            nc.vector.memset(running, 1.0).then_inc(zeroed, 1)
            nc.vector.memset(reset, RESET).then_inc(zeroed, 1)
            for s in range(G):
                build_sel(0, 0, s)
            dve.wait_ge(zeroed, 4)
            rectify(0, 0)
            over_iterations(dve, body)

    nc.clear_and_free_semaphores(sems)
    nc.all_engine_barrier()


def dense(nc, a, m, layer, xl_table, out):
    final = out is not None
    ctx = ExitStack()
    with ctx:
        def sem(name):
            return ctx.enter_context(nc.semaphore(f"d{layer}_{name}"))

        area = Area(m["work"])
        B = BT * P
        h = area.take(B)
        h_b2 = [area.take(B) for _ in range(2)]
        hT = area.take(B)
        u = [area.take(FB * Q * P).rearrange("p (f n) -> p f n", f=FB) for _ in range(2)]
        y = [area.take(B) for _ in range(2)]
        w1 = area.take(F)
        w2 = area.take(F).rearrange("p (f d) -> p f d", f=FB)
        b1 = area.take(FB)
        rows = area.take(4 * D).rearrange("p (k d) -> p k d", k=4)
        den = area.take(BT * H)
        stats = area.take(BT * 6)
        norm = area.take(BT * 2)
        dev = area.take(BT)
        eps = area.take(1)
        if final:
            x_beta = [area.take(B) for _ in range(2)]
        else:
            yT = area.take(B)
            both = [area.take(BT * 2 * D) for _ in range(2)]
        turn_ps = ctx.enter_context(nc.psum_tensor(f"d{layer}_t", [P, 512], F32))
        u_ps = [ctx.enter_context(nc.psum_tensor(f"d{layer}_u{i}", [P, 512], F32)) for i in range(3)]
        y_ps = [ctx.enter_context(nc.psum_tensor(f"d{layer}_y{i}", [P, 512], F32)) for i in range(2)]
        p_ps = [ctx.enter_context(nc.psum_tensor(f"d{layer}_p{i}", [P, 512], F32)) for i in range(2)]
        HALVES = ((0, Q), (Q, BT))
        PAIRS = -(-BT // 2)

        names = ("weights_in", "h_made", "h_b2_made", "turned", "turn_kept", "u_made", "u_kept", "y_made", "y_added",
                 "chain", "normed", "var_made", "dev_made", "projected", "added", "hi", "rest1", "mid", "low", "x_beta_made", "passed", "h_chain")
        (weights_in, h_made, h_b2_made, turned, turn_kept, u_made, u_kept, y_made, y_added, chain, normed, var_made, dev_made,
         projected, added, hi, rest1, mid, low, x_beta_made, passed, h_chain) = (sem(s) for s in names)
        x_in, stored = ([sem(f"{s}{b}") for b in range(2)] for s in ("x_in", "stored"))
        CHAIN = 7 if final else 4
        NORMS = 2 if final else 1
        H_CHAIN = 3
        LOADS = 16 * (7 + (0 if final else 4 + H))
        block = ctx.enter_context(nc.Block())
        x3 = parts_view(m)
        sums3 = m["sums"][:, :].rearrange("p (t w) -> p t w", w=W)
        f_, l_ = f"f{layer}_", f"ln{layer}_"

        def tiles_of(v):
            return v.rearrange("p (t d) -> p t d", t=BT)

        def rows_of(dram, k):
            return dram[bass.ds(k * B, B), :].rearrange("(t p) d -> p t d", p=P)

        def h_turn(j, n):
            if final or isinstance(j, int) and j < 2:
                return j * 2 + (n + 1)
            return (j - 1) * 4 + (4 if n else 1)

        def y_turn(j, n):
            if isinstance(j, int) and j == BATCHES - 1:
                return (BATCHES - 1) * 4 + 3 + n
            return (j + 1) * 4 + (n + (1 if isinstance(j, int) and j == BATCHES - 2 else 2))

        def over_batches(eng, body):
            body(0, 0, 0, before=False)
            body(1, 0, 1)
            with eng.Fori(0, BATCHES // 2 - 2) as it:
                for b in range(2):
                    body(it * 2 + (2 + b), it + 1, b)
            body(BATCHES - 2, BATCHES // 2 - 1, 0, after2=False)
            body(BATCHES - 1, BATCHES // 2 - 1, 1, after=False, after2=False)
            body(BATCHES, BATCHES // 2, 0, new=False, after=False, after2=False)

        @block.sync
        def _(sp):
            sp.dma_start(w1, a[f_ + "w1"]).then_inc(weights_in, 16)
            sp.dma_start(w2, a[f_ + "w2"].rearrange("(f p) d -> p f d", p=P)).then_inc(weights_in, 16)
            sp.dma_start(b1, a[f_ + "b1"]).then_inc(weights_in, 16)
            for k, name in enumerate((f"c{layer}_bias", f_ + "b2", l_ + "g", l_ + "b")):
                sp.dma_start(rows[:, k, :], a[name].partition_broadcast(P)).then_inc(weights_in, 16)
            if not final:
                load_projection(sp, a, m, 2, weights_in)
            if final:
                for k in range(2):
                    sp.dma_start(tiles_of(x_beta[k]), rows_of(a["x"], k)).then_inc(x_in[k], 16)

            def body(k, r, b, before=True, new=True, after=True, after2=True):
                if final and new:
                    sp.wait_ge(normed, k + 1)
                    sp.dma_start(rows_of(out, k), tiles_of(y[b])).then_inc(stored[b], 16)
                    if after2:
                        sp.dma_start(tiles_of(x_beta[b]), rows_of(a["x"], k + 2)).then_inc(x_in[b], 16)
                elif not final and before:
                    sp.wait_ge(added, k * PAIRS)
                    sp.dma_start(rows_of(xl_table, k - 1), tiles_of(both[1 - b])[:, :, 0:D]).then_inc(stored[1 - b], 16)

            over_batches(sp, body)
            for b in range(2):
                sp.wait_ge(stored[b], BATCHES // 2 * 16)

        @block.gpsimd
        def _(pool):
            def add_b2(k, b):
                pool.wait_ge(h_made, k + 1)
                nc.gpsimd.tensor_tensor(tiles_of(h_b2[b]), tiles_of(h), rows[:, 1, :].unsqueeze(1).to_broadcast(
                    [P, BT, D]), ALU.add).then_inc(h_b2_made, 1)

            def add_beta(k, r, b):
                pool.wait_ge(x_in[b], r * 16 + 16)
                nc.gpsimd.tensor_tensor(tiles_of(x_beta[b]), tiles_of(x_beta[b]), rows[:, 3, :].unsqueeze(1).to_broadcast(
                    [P, BT, D]), ALU.add).then_inc(x_beta_made, 1)

            def split(j, b):
                rest = tiles_of(both[b])[:, :, D:2 * D]
                tiles = bass.ds(j * BT, BT)
                hold(pool, added, j * PAIRS + PAIRS, passed)
                nc.gpsimd.tensor_copy(x3[:, tiles, 0, :], rest).then_inc(hi, 1)
                hold(pool, hi, j + 1, passed)
                nc.gpsimd.tensor_tensor(rest, rest, x3[:, tiles, 0, :], ALU.subtract).then_inc(rest1, 1)
                hold(pool, rest1, j + 1, passed)
                nc.gpsimd.tensor_copy(x3[:, tiles, 1, :], rest).then_inc(mid, 1)
                hold(pool, mid, j + 1, passed)
                nc.gpsimd.tensor_tensor(x3[:, tiles, 2, :], rest, x3[:, tiles, 1, :], ALU.subtract).then_inc(low, 1)

            def body(k, r, b, before=True, new=True, after=True, after2=True):
                if before and not final:
                    split(k - 1, 1 - b)
                if after2:
                    add_b2(k + 2, b)
                    if final:
                        add_beta(k + 2, r + 1, b)

            pool.wait_ge(weights_in, LOADS)
            for k in range(2):
                add_b2(k, k)
                if final:
                    add_beta(k, 0, k)
            over_batches(pool, body)

        @block.tensor
        def _(pe):
            ident = m["ident"][:, :]
            pe.wait_ge(weights_in, LOADS)

            def turn(src, n, count):
                wait(pe, turn_kept, count - 1)
                lo, hi_ = HALVES[n]
                for j in range(lo, hi_):
                    i = nc.tensor.transpose(turn_ps[:, (j - lo) * P:(j - lo + 1) * P], src[:, j * P:(j + 1) * P], ident)
                i.then_inc(turned, 1)

            def first(k, n):
                lo, hi_ = HALVES[n]
                pe.wait_ge(turn_kept, h_turn(k, n))
                for f in range(FB):
                    i = n * FB + f
                    before = (k * 2 * FB + (i - 2)) if i >= 3 else (k - 1) * 2 * FB + (6 if i == 2 else 7 + i)
                    wait(pe, u_kept, before)
                    nc.tensor.matmul(u_ps[i % 3][:, 0:(hi_ - lo) * P], w1[:, f * P:(f + 1) * P],
                                     hT[:, lo * P:hi_ * P], start=True, stop=True).then_inc(u_made, 1)

            def second(k, n):
                lo, hi_ = HALVES[n]
                wait(pe, y_added, (k - 1) * 2 + (n + 1))
                pe.wait_ge(u_kept, k * 2 * FB + (n * FB + FB))
                for j in range(lo, hi_):
                    at = slice((j - lo) * P, (j - lo + 1) * P)
                    for f in range(FB):
                        i = nc.tensor.matmul(y_ps[n][:, at], u[n][:, f, at], w2[:, f, :],
                                             start=(f == 0), stop=(f == FB - 1))
                i.then_inc(y_made, 1)

            def project(j, p):
                wait(pe, added, j * PAIRS + (p - 1))
                pe.wait_ge(turn_kept, y_turn(j, 0 if p < 2 else 1))
                for t in range(2 * p, min(2 * p + 2, BT)):
                    i = nc.tensor.matmul(p_ps[p % 2][:, (t % 2) * 2 * D:(t % 2 + 1) * 2 * D], yT[:, t * P:(t + 1) * P],
                                         m["wproj"][:, :], start=True, stop=True)
                i.then_inc(projected, 1)

            def body(k, r, b, before=True, new=True, after=True, after2=True):
                before = before and not final
                if new:
                    first(k, 0)
                if after:
                    pe.wait_ge(h_made, k + 2)
                    turn(h, 0, h_turn(k + 1, 0))
                if new:
                    second(k, 0)
                    first(k, 1)
                if before:
                    hold(pe, normed, k, passed)
                    turn(y[1 - b], 0, y_turn(k - 1, 0))
                if new:
                    second(k, 1)
                if before:
                    turn(y[1 - b], 1, y_turn(k - 1, 1))
                    project(k - 1, 0)
                    project(k - 1, 1)
                if after:
                    turn(h, 1, h_turn(k + 1, 1))
                if before:
                    project(k - 1, 2)
                    project(k - 1, 3)

            pe.wait_ge(h_made, 1)
            turn(h, 0, 1)
            turn(h, 1, 2)
            over_batches(pe, body)

        @block.scalar
        def _(act):
            act.wait_ge(weights_in, LOADS)

            def keep(to, n, count):
                lo, hi_ = HALVES[n]
                act.wait_ge(turned, count)
                nc.scalar.copy(to[:, lo * P:hi_ * P], turn_ps[:, 0:(hi_ - lo) * P]).then_inc(turn_kept, 1)

            def relu(k, n):
                lo, hi_ = HALVES[n]
                for f in range(FB):
                    i = n * FB + f
                    act.wait_ge(u_made, k * 2 * FB + (i + 1))
                    nc.scalar.activation(u[n][:, f, 0:(hi_ - lo) * P], u_ps[i % 3][:, 0:(hi_ - lo) * P], ACT.Relu,
                                         bias=b1[:, f:f + 1]).then_inc(u_kept, 1)

            def deviate(j, r):
                act.wait_ge(var_made, j * NORMS + (r + 1))
                nc.scalar.activation(dev, norm[:, 1:2 * BT:2], ACT.Sqrt, bias=eps).then_inc(dev_made, 1)

            def body(k, r, b, before=True, new=True, after=True, after2=True):
                if new:
                    relu(k, 0)
                if after:
                    keep(hT, 0, h_turn(k + 1, 0))
                if before:
                    deviate(k - 1, 0)
                if new:
                    relu(k, 1)
                if before and final:
                    deviate(k - 1, 1)
                if before and not final:
                    keep(yT, 0, y_turn(k - 1, 0))
                    keep(yT, 1, y_turn(k - 1, 1))
                if after:
                    keep(hT, 1, h_turn(k + 1, 1))

            keep(hT, 0, 1)
            keep(hT, 1, 2)
            over_batches(act, body)

        @block.vector
        def _(dve):
            nc.vector.memset(eps, EPS)
            dve.wait_ge(weights_in, LOADS)
            norm3 = norm.rearrange("p (t k) -> p t k", k=2)
            den3 = den.rearrange("p (t h) -> p t h", h=H)

            def all_tiles(k):
                return rows[:, k, :].unsqueeze(1).to_broadcast([P, BT, D])

            def make_h(k):
                done = [0]

                def link(ins):
                    done[0] += 1
                    ins.then_inc(h_chain, 1)
                    dve.wait_ge(h_chain, k * H_CHAIN + done[0])

                sums = sums3[:, bass.ds(k * BT, BT), :]
                link(nc.vector.tensor_scalar(den3, sums[:, :, D:W], 1e-16, None, ALU.add))
                link(nc.vector.reciprocal(den, den))
                wait(dve, h_b2_made, k)
                wait(dve, turned, h_turn(k - 1, 1))
                link(nc.vector.tensor_tensor(
                    h.rearrange("p (t h c) -> p t h c", t=BT, h=H),
                    sums[:, :, 0:D].rearrange("p t (h c) -> p t h c", h=H),
                    den3.unsqueeze(3).to_broadcast([P, BT, H, C]), ALU.mult))
                nc.vector.tensor_tensor(tiles_of(h), tiles_of(h), all_tiles(0), ALU.add).then_inc(h_made, 1)

            def body(k, r, b, before=True, new=True, after=True, after2=True):
                done = [0]
                yb, y3 = y[b], tiles_of(y[b])

                def link(ins):
                    done[0] += 1
                    ins.then_inc(chain, 1)
                    dve.wait_ge(chain, k * CHAIN + done[0])

                def standardize(nth):
                    for j in range(BT):
                        i = nc.vector.bn_stats(stats[:, j * 6:(j + 1) * 6], y3[:, j, :])
                    link(i)
                    dve.sem_inc(passed, 1)
                    for j in range(BT):
                        i = nc.vector.bn_aggr(norm3[:, j, :], stats[:, j * 6:(j + 1) * 6])
                    i.then_inc(var_made, 1)
                    dve.wait_ge(var_made, k * NORMS + (nth + 1))
                    dve.wait_ge(dev_made, k * NORMS + (nth + 1))
                    link(nc.vector.reciprocal(dev, dev))
                    for j in range(BT):
                        i = nc.vector.tensor_scalar(y3[:, j, :], y3[:, j, :], norm3[:, j, 0:1], dev[:, j:j + 1],
                                                    ALU.subtract, ALU.mult)
                    return i

                if new:
                    if final:
                        wait(dve, stored[b], r * 16)
                    dve.wait_ge(h_b2_made, k + 1)
                    for n, (lo, hi_) in enumerate(HALVES):
                        dve.wait_ge(y_made, k * 2 + (n + 1))
                        nc.vector.tensor_tensor(yb[:, lo * P:hi_ * P], y_ps[n][:, 0:(hi_ - lo) * P],
                                                h_b2[b][:, lo * P:hi_ * P], ALU.add).then_inc(y_added, 1)
                if before and not final:
                    j = k - 1
                    wait(dve, stored[1 - b], (r if b else r - 1) * 16)
                    wait(dve, low, j - 1)
                    for p in range(PAIRS):
                        dve.wait_ge(projected, j * PAIRS + (p + 1))
                        t = min(2, BT - 2 * p)
                        nc.vector.tensor_tensor(
                            tiles_of(both[1 - b])[:, 2 * p:2 * p + t, :],
                            p_ps[p % 2][:, 0:t * 2 * D].rearrange("p (t d) -> p t d", t=t),
                            m["bproj"][:, :].unsqueeze(1).to_broadcast([P, t, 2 * D]), ALU.add).then_inc(added, 1)
                if after2:
                    make_h(k + 2)
                if new:
                    dve.wait_ge(y_added, k * 2 + 2)
                    link(standardize(0))
                    link(nc.vector.tensor_tensor(y3, y3, all_tiles(2), ALU.mult))
                    if final:
                        dve.wait_ge(x_beta_made, k + 1)
                        link(nc.vector.tensor_tensor(yb, yb, x_beta[b], ALU.add))
                        standardize(1).then_inc(normed, 1)
                    else:
                        nc.vector.tensor_tensor(y3, y3, all_tiles(3), ALU.add).then_inc(normed, 1)
                    assert done[0] == CHAIN, done[0]

            make_h(0)
            make_h(1)
            over_batches(dve, body)


def kernel(**inputs):
    import numpy as np
    import concourse.bacc as bacc
    from concourse.bass_utils import run_bass_kernel_spmd

    given = {k.removeprefix("L0_gnn_"): np.asarray(v) for k, v in inputs.items()}
    x = np.zeros((NP, D), np.float32)
    x[:N] = given["x"]
    src = np.zeros(((CHUNKS + 1) * P,), np.int32)
    dst = np.full(((CHUNKS + 1) * P,), NP - 1, np.int32)
    src[:E], dst[:E] = given["src"], given["dst"]
    src, dst = src.reshape(-1, P), dst.reshape(-1, P)
    arrays = {"x": x, "xT": np.ascontiguousarray(x.T), "src_chunks": src, "dst_chunks": dst,
              "last_dst": np.ascontiguousarray(dst[:CHUNKS, P - 1])}
    for k, v in given.items():
        if k in ("x", "src", "dst"):
            continue
        if k.endswith("_att"):
            v = v.reshape(H * C, 1)
        elif k.endswith("_b1"):
            v = np.ascontiguousarray(v.reshape(FB, P).T)
        arrays[k] = v

    nc = bacc.Bacc("TRN2", target_bir_lowering=False, num_devices=1)
    a = {k: nc.dram_tensor("in_" + k, v.shape, mybir.dt.from_np(v.dtype), kind="ExternalInput").ap()
         for k, v in arrays.items()}
    out = nc.dram_tensor("out", [NP, D], F32, kind="ExternalOutput").ap()
    build(nc, a, out)
    r = run_bass_kernel_spmd(nc, [{"in_" + k: v for k, v in arrays.items()}], core_ids=[0])
    return r.results[0]["out"][:N]
```
